# Optimizing a Trainium2 kernel written in Bass

```python
import numpy as np
import jax
import jax.numpy as jnp

def _softmax(x, axis=-1):
    return jax.nn.softmax(x, axis=axis)

def _gelu(x):
    return jax.nn.gelu(x, approximate=True)

def _silu(x):
    return jax.nn.silu(x)

def _sigmoid(x):
    return jax.nn.sigmoid(x)

def _layernorm(x, axis=-1, eps=1e-05):
    m = jnp.mean(x, axis=axis, keepdims=True)
    v = jnp.var(x, axis=axis, keepdims=True)
    return (x - m) / jnp.sqrt(v + eps)

def _scatter_add(tgt, idx, src, axis=0):
    return tgt.at[idx].add(src)

def _segment_sum(src, seg, n):
    return jax.ops.segment_sum(src, seg, n)
kernel_name = 'mk_prb_d1_jaxref_r8_58ccf2'

def setup_inputs(seed: int=0):
    np.random.seed(seed)
    _w = jnp.asarray

    def _L0_attn_setup():
        import jax, jax.numpy as jnp
        import numpy as np
        B, S, D = (2, 256, 256)
        N_HEADS, N_KV_HEADS = (16, 4)
        HEAD_DIM = D // N_HEADS

        def _apply_rope(xh, positions):
            Dh = xh.shape[-1]
            half = Dh // 2
            freqs = 1.0 / 10000.0 ** (jnp.arange(half, dtype=jnp.float32) / half)
            angles = positions[:, None].astype(jnp.float32) * freqs[None, :]
            cos, sin = (jnp.cos(angles), jnp.sin(angles))
            xp = xh.reshape(*xh.shape[:-1], half, 2)
            x0, x1 = (xp[..., 0], xp[..., 1])
            r0 = x0 * cos - x1 * sin
            r1 = x0 * sin + x1 * cos
            return jnp.stack([r0, r1], axis=-1).reshape(xh.shape)
        key = jax.random.key(seed)
        ks = jax.random.split(key, 5)
        x = jax.random.normal(ks[0], (B, S, D), dtype=jnp.float32)
        W_q = jax.random.normal(ks[1], (D, D), dtype=jnp.float32) * 0.02
        W_k = jax.random.normal(ks[2], (D, N_KV_HEADS * HEAD_DIM), dtype=jnp.float32) * 0.02
        W_v = jax.random.normal(ks[3], (D, N_KV_HEADS * HEAD_DIM), dtype=jnp.float32) * 0.02
        W_o = jax.random.normal(ks[4], (D, D), dtype=jnp.float32) * 0.02
        return {'x': x, 'W_q': W_q, 'W_k': W_k, 'W_v': W_v, 'W_o': W_o}
    _L0_attn_in = _L0_attn_setup()

    def _L0_ffn_setup():
        import jax, jax.numpy as jnp
        import numpy as np
        NUM_EXPERTS = 8
        TOP_K = 2
        HIDDEN = 256
        INTER = 256
        SWIGLU_LIMIT = 7.0
        BATCH, SEQ = (4, 256)
        key = jax.random.key(seed)
        k0, k1, k2, k3, k4 = jax.random.split(key, 5)
        x = jax.random.normal(k0, (BATCH, SEQ, HIDDEN), jnp.float32)
        Wr = jax.random.normal(k1, (HIDDEN, NUM_EXPERTS), jnp.float32) * 0.02
        Wg = jax.random.normal(k2, (NUM_EXPERTS, HIDDEN, INTER), jnp.float32) * 0.02
        Wu = jax.random.normal(k3, (NUM_EXPERTS, HIDDEN, INTER), jnp.float32) * 0.02
        Wd = jax.random.normal(k4, (NUM_EXPERTS, INTER, HIDDEN), jnp.float32) * 0.02
        return {'hidden_states': x, 'Wr': Wr, 'Wg': Wg, 'Wu': Wu, 'Wd': Wd}
    _L0_ffn_in = _L0_ffn_setup()
    _d = {'L0_attn_x': _L0_attn_in['x'], 'L0_attn_W_q': _L0_attn_in['W_q'], 'L0_attn_W_k': _L0_attn_in['W_k'], 'L0_attn_W_v': _L0_attn_in['W_v'], 'L0_attn_W_o': _L0_attn_in['W_o'], 'L0_ffn_Wr': _L0_ffn_in['Wr'], 'L0_ffn_Wg': _L0_ffn_in['Wg'], 'L0_ffn_Wu': _L0_ffn_in['Wu'], 'L0_ffn_Wd': _L0_ffn_in['Wd']}
    _x0 = _d['L0_attn_x']
    _d['L0_attn_x'] = jax.random.normal(jax.random.fold_in(jax.random.key(seed), 1), (2, 1024, 256), dtype=_x0.dtype)
    del _x0
    return _d

def reference(L0_attn_x, L0_attn_W_q, L0_attn_W_k, L0_attn_W_v, L0_attn_W_o, L0_ffn_Wr, L0_ffn_Wg, L0_ffn_Wu, L0_ffn_Wd):

    def _L0_attn_ref(x, W_q, W_k, W_v, W_o):
        import jax, jax.numpy as jnp
        import numpy as np
        B, S, D = (2, 256, 256)
        N_HEADS, N_KV_HEADS = (16, 4)
        HEAD_DIM = D // N_HEADS

        def _apply_rope(xh, positions):
            Dh = xh.shape[-1]
            half = Dh // 2
            freqs = 1.0 / 10000.0 ** (jnp.arange(half, dtype=jnp.float32) / half)
            angles = positions[:, None].astype(jnp.float32) * freqs[None, :]
            cos, sin = (jnp.cos(angles), jnp.sin(angles))
            xp = xh.reshape(*xh.shape[:-1], half, 2)
            x0, x1 = (xp[..., 0], xp[..., 1])
            r0 = x0 * cos - x1 * sin
            r1 = x0 * sin + x1 * cos
            return jnp.stack([r0, r1], axis=-1).reshape(xh.shape)
        b, s, d = x.shape
        positions = jnp.arange(s)
        rep = N_HEADS // N_KV_HEADS
        Q = (x @ W_q).reshape(b, s, N_HEADS, HEAD_DIM).transpose(0, 2, 1, 3)
        K = (x @ W_k).reshape(b, s, N_KV_HEADS, HEAD_DIM).transpose(0, 2, 1, 3)
        V = (x @ W_v).reshape(b, s, N_KV_HEADS, HEAD_DIM).transpose(0, 2, 1, 3)
        Qr = _apply_rope(Q, positions)
        K_rep = jnp.tile(K, (1, rep, 1, 1))
        V_rep = jnp.tile(V, (1, rep, 1, 1))
        Kr = _apply_rope(K_rep, positions)
        scores = jnp.einsum('bhqd,bhkd->bhqk', Qr, Kr) / HEAD_DIM ** 0.5
        weights = jax.nn.softmax(scores, axis=-1)
        out = jnp.einsum('bhqk,bhkd->bhqd', weights, V_rep)
        out = out.transpose(0, 2, 1, 3).reshape(b, s, d)
        return out @ W_o

    def _L0_ffn_ref(hidden_states, Wr, Wg, Wu, Wd):
        import jax, jax.numpy as jnp
        import numpy as np
        NUM_EXPERTS = 8
        TOP_K = 2
        HIDDEN = 256
        INTER = 256
        SWIGLU_LIMIT = 7.0
        BATCH, SEQ = (4, 256)
        router_logits = jnp.einsum('bsh,he->bse', hidden_states, Wr)
        topk_logits, selected = jax.lax.top_k(router_logits, TOP_K)
        router_probs = jax.nn.softmax(topk_logits, axis=-1)
        out = jnp.zeros_like(hidden_states)
        for e in range(NUM_EXPERTS):
            w_e = jnp.where(selected == e, router_probs, 0.0).sum(axis=-1, keepdims=True)
            g = jnp.einsum('bsh,hi->bsi', hidden_states, Wg[e])
            g = jnp.clip(jax.nn.silu(g), -SWIGLU_LIMIT, SWIGLU_LIMIT)
            u = jnp.einsum('bsh,hi->bsi', hidden_states, Wu[e])
            h = jnp.einsum('bsi,ih->bsh', g * u, Wd[e])
            out = out + h * w_e
        return out
    x = L0_attn_x
    xn = _layernorm(x, axis=-1)
    x = x + _L0_attn_ref(xn, L0_attn_W_q, L0_attn_W_k, L0_attn_W_v, L0_attn_W_o) + _L0_ffn_ref(xn, L0_ffn_Wr, L0_ffn_Wg, L0_ffn_Wu, L0_ffn_Wd)
    return x

_drawn_inputs = setup_inputs


def setup_inputs(seed=0):
    import zlib

    import numpy as np

    out = dict(_drawn_inputs(seed))
    spreads = {}
    factors = {'L0_attn_W_q': 8.0,
     'L0_attn_W_k': 8.0,
     'L0_attn_W_v': 8.0,
     'L0_attn_W_o': 8.0,
     'L0_ffn_Wr': 5.458,
     'L0_ffn_Wg': 4.736,
     'L0_ffn_Wu': 4.683,
     'L0_ffn_Wd': 4.686}
    for name, (base, spread) in spreads.items():
        noise = np.random.default_rng([zlib.crc32(name.encode()), seed]).standard_normal(out[name].shape)
        drawn = base * np.exp(spread * noise) if base else spread * noise
        out[name] = jnp.asarray(drawn.astype(out[name].dtype))
    for name, factor in factors.items():
        out[name] = (out[name] * factor).astype(out[name].dtype)
    return out
```

```python
import math
from contextlib import ExitStack

import numpy as np

import concourse.bass as bass
from concourse import mybir

F32 = mybir.dt.float32
F32R = mybir.dt.float32r
I32 = mybir.dt.int32
U32 = mybir.dt.uint32
ALU = mybir.AluOpType
ACT = mybir.ActivationFunctionType
X_AXIS = mybir.AxisListType.X

P = 128
HD = 16
LN_EPS = 1e-5
CLAMP = 7.0
FAR = 3.0e38


def build(nc, x, w_q, w_k, w_v, w_o, w_r, w_g, w_u, w_d, cos_t, sin_t, out):
    B, S, D = x.shape
    C = D // P
    NH = w_q.shape[1] // HD
    KV = w_k.shape[1] // HD
    R = NH // KV
    E, _, F = w_g.shape
    NT = B * S // P
    ST_T = S // P
    G = B * KV
    HALF = S // 2
    KT = S // P
    QT = HALF // P
    TB = 4
    STACK = 4 * HD
    AUG = STACK + 2
    SLOTS = 2 * NT + E
    NA = R * QT * 2
    TURN = 4
    NI = NA + 1
    assert C == 2 and R == 4 and KT == 8 and QT == 4 and E == 8 and HALF == 512 and F == 256
    assert B == 2 and TB * P == HALF

    xt = x.rearrange("b (t p) d -> p (b t) d", p=P)
    out_t = out.rearrange("b (t p) d -> p (b t) d", p=P)

    q_hl = nc.dram_tensor("q_hl", [B, NH, 2 * HD, S], F32, kind="Internal").ap()
    k_st = nc.dram_tensor("k_st", [B, KV, STACK, S], F32, kind="Internal").ap()
    rows_in = nc.dram_tensor("rows_in", [SLOTS * P, D], F32, kind="Internal").ap()
    rows_out = nc.dram_tensor("rows_out", [SLOTS * P, D], F32, kind="Internal").ap()

    with ExitStack() as ctx:
        def sb(name, shape, dt=F32):
            return ctx.enter_context(nc.sbuf_tensor(name, shape, dt))

        def sem(name):
            return ctx.enter_context(nc.semaphore(name))

        big = sb("big", [P, E * C * 3 * F])
        wgu = big[:, 0:E * C * 2 * F].rearrange("p (e c n) -> p e c n", e=E, c=C)
        wdn = big[:, E * C * 2 * F:].rearrange("p (e c n) -> p e c n", e=E, c=C)
        attn_t = big[:, 0:KV * B * S].rearrange("p (k t) -> p k t", k=KV)
        probs = [big[:, KV * B * S + i * R * HALF:KV * B * S + (i + 1) * R * HALF]
                 .rearrange("p (r q) -> p r q", r=R) for i in range(2)]
        xs = sb("xs", [P, NT, D])
        xn = sb("xn", [P, NT, D])
        xn_t = [sb(f"xn_t{h}", [P, C, HALF]) for h in range(2)]
        wqk = sb("wqk", [P, C, (NH + KV) * HD])
        wvr = sb("wvr", [P, C, KV * HD + E])
        wo_s = sb("wo_s", [P, KV, D])
        cos_s = sb("cos_s", [P, S])
        sin_s = sb("sin_s", [P, S])
        rope_a = [sb(f"rope_a{m}", [P, HALF]) for m in range(3)]
        rope_b = [sb(f"rope_b{m}", [P, HALF]) for m in range(3)]
        rope_hi = [sb(f"rope_hi{m}", [P, HALF], F32R) for m in range(3)]
        rope_lo = [sb(f"rope_lo{m}", [P, HALF], F32R) for m in range(3)]
        stats = [sb(f"stats{h}", [P, TB, 6]) for h in range(2)]
        mean_var = [sb(f"mean_var{h}", [P, TB, 2]) for h in range(2)]
        std = [sb(f"std{h}", [P, TB]) for h in range(2)]
        rstd = [sb(f"rstd{h}", [P, TB]) for h in range(2)]
        eps = sb("eps", [P, 1])
        v_all = sb("v_all", [P, NT, KV * HD])
        ident = sb("ident", [P, P])
        earlier = sb("earlier", [P, P])
        ones = sb("ones", [P, P])
        zeros = sb("zeros", [P, D])
        logits = sb("logits", [P, NT, E])
        logits2 = sb("logits2", [P, NT, E])
        expert_no = sb("expert_no", [P, 2 * NT, E])
        cand = sb("cand", [P, NT, E])
        top = sb("top", [P, 2, NT])
        choice = sb("choice", [P, 2, NT])
        onehot = sb("onehot", [P, 2, NT, E])
        gate = sb("gate", [P, 2, NT])
        gate_t = sb("gate_t", [P, 3, NT])
        sums = [sb(f"sums{i}", [P, 2 * NT, E]) for i in range(2)]
        totals = sb("totals", [P, 2 * NT, E])
        limit = sb("limit", [P, E, NT])
        over = sb("over", [P, E, NT])
        n_tiles = sb("n_tiles", [P, E])
        cum = [sb(f"cum{i}", [P, E]) for i in range(2)]
        slot_no = sb("slot_no", [P, SLOTS, E])
        slot_ge = sb("slot_ge", [P, SLOTS, E])
        slot_e = sb("slot_e", [P, SLOTS])
        slot_ei = sb("slot_ei", [P, SLOTS], I32)
        place = sb("place", [P, 2 * NT])
        place_i = sb("place_i", [P, 2 * NT], U32)
        spare = xn[:, :, :].rearrange("p t d -> p (t d)")

        def in_spare(n, width):
            return spare[:, n * width:(n + 1) * width]

        rows = [in_spare(i, D) for i in range(4)]
        rows_t = [in_spare(4 + i, D).rearrange("p (c n) -> p c n", c=C) for i in range(2)]
        act_g = [in_spare(6 + i, F) for i in range(2)]
        act_h = [in_spare(8 + i, F) for i in range(2)]
        act_t = [in_spare(10 + i, F).rearrange("p (c n) -> p c n", c=C) for i in range(2)]
        y_s = [in_spare(12 + i, D) for i in range(4)]
        o_q = in_spare(2, HALF)
        o_n = in_spare(3, HALF)
        o_t = [in_spare(h, HALF) for h in range(2)]
        qa = [sb(f"qa{h}", [P, R, HALF], F32R) for h in range(2)]
        qb = [sb(f"qb{h}", [P, R, HALF], F32R) for h in range(2)]
        ka = [sb(f"ka{p}", [P, S], F32R) for p in range(2)]
        kb = [sb(f"kb{p}", [P, S], F32R) for p in range(2)]
        v_st = [sb(f"v_st{p}", [P, KT, 32]) for p in range(2)]
        mx = [sb(f"mx{h}", [P, R * QT, 2]) for h in range(2)]
        neg_mx = sb("neg_mx", [P, R * QT])
        m_hi = [sb(f"m_hi{h}", [R * QT, P], F32R) for h in range(2)]
        m_lo = [sb(f"m_lo{h}", [R * QT, P], F32R) for h in range(2)]
        rden = sb("rden", [P, HALF // 32])
        y_got = [rope_a[0][:, k * D:(k + 1) * D] for k in range(2)]
        fin = [rope_a[1][:, k * D:(k + 1) * D] for k in range(2)]
        attn_c = [rope_b[i][:, :].rearrange("p (k n) -> p k n", k=KV) for i in range(2)]

        bank = [ctx.enter_context(nc.psum_tensor(f"bank{i}", [P, 1024], F32)) for i in range(4)]

        def half_bank(i):
            return bank[i // 2][:, 512 * (i % 2):512 * (i % 2) + 512]

        tr_ps = [half_bank(0), half_bank(1)]
        vr_ps = half_bank(2)
        pj_ps = [half_bank(3), half_bank(4), half_bank(5)]
        rank_ps = half_bank(6)
        total_ps = half_bank(7)
        xt_ps = [half_bank(0), half_bank(1)]
        gu_ps = [half_bank(2), half_bank(3)]
        ht_ps = [half_bank(4), half_bank(5)]
        y_ps = [half_bank(6), half_bank(7)]
        st_ps = [bank[0], bank[1]]
        mx_ps = [half_bank(4), half_bank(5), half_bank(6)]
        o_ps = half_bank(7)
        wo_ps = [half_bank(0), half_bank(1)]

        x_loaded = [sem(f"x_loaded{h}") for h in range(2)]
        small_loaded = sem("small_loaded")
        wo_loaded = sem("wo_loaded")
        experts_loaded = sem("experts_loaded")
        rows_zeroed = sem("rows_zeroed")
        pool_made = sem("pool_made")
        vec_made = sem("vec_made")
        stacks_padded = sem("stacks_padded")
        dve_ln = sem("dve_ln")
        stats_ready = sem("stats_ready")
        std_ready = sem("std_ready")
        xn_ready = sem("xn_ready")
        tr_ready = sem("tr_ready")
        xn_t_ready = sem("xn_t_ready")
        vr_ready = sem("vr_ready")
        vr_taken = sem("vr_taken")
        pj_ready = sem("pj_ready")
        pj_taken = sem("pj_taken")
        swapped = sem("swapped")
        cos_done = sem("cos_done")
        sin_done = sem("sin_done")
        rope_done = sem("rope_done")
        hi_ready = sem("hi_ready")
        lo_ready = sem("lo_ready")
        qk_stored = [sem(f"qk_stored{m}") for m in range(3)]
        route = sem("route")
        choices_ready = sem("choices_ready")
        counts_ready = sem("counts_ready")
        diff_ready = sem("diff_ready")
        gate_exp = sem("gate_exp")
        gates_ready = sem("gates_ready")
        places_ready = sem("places_ready")
        scattered = sem("scattered")
        rows_loaded = [sem(f"rows_loaded{i}") for i in range(4)]
        xt_ready = sem("xt_ready")
        rows_t_ready = sem("rows_t_ready")
        gu_ready = sem("gu_ready")
        silu_ready = sem("silu_ready")
        clip_done = sem("clip_done")
        act_ready = sem("act_ready")
        ht_ready = sem("ht_ready")
        act_t_ready = sem("act_t_ready")
        y_ready = sem("y_ready")
        y_copied = sem("y_copied")
        y_stored = [sem(f"y_stored{i}") for i in range(4)]
        qa_loaded = [sem(f"qa_loaded{h}") for h in range(2)]
        qb_loaded = [sem(f"qb_loaded{h}") for h in range(2)]
        ka_loaded = [sem(f"ka_loaded{p}") for p in range(2)]
        kb_loaded = [sem(f"kb_loaded{p}") for p in range(2)]
        v_staged = sem("v_staged")
        mx_scored = sem("mx_scored")
        mx_taken = sem("mx_taken")
        neg_mx_ready = sem("neg_mx_ready")
        m_hi_ready = sem("m_hi_ready")
        st_ready = sem("st_ready")
        exp_done = sem("exp_done")
        products_done = sem("products_done")
        o_free = sem("o_free")
        rden_ready = sem("rden_ready")
        divided = sem("divided")
        attn_ready = sem("attn_ready")
        o_t_free = sem("o_t_free")
        y_gathered = sem("y_gathered")
        mix = sem("mix")
        mixed = sem("mixed")
        attn_copied = sem("attn_copied")
        wo_ready = sem("wo_ready")
        fin_ready = sem("fin_ready")
        stored = [sem(f"stored{i}") for i in range(2)]

        def uses_before(v):
            return NI * v - 1

        block = ctx.enter_context(nc.Block())

        @block.sync
        def _(sp):
            def load_x(b, h):
                t0 = b * ST_T + h * TB
                sp.dma_start(xs[:, t0:t0 + TB, :], xt[:, t0:t0 + TB, :]).then_inc(x_loaded[h], 16)

            load_x(0, 0)
            load_x(0, 1)
            for b in range(1, B):
                for h in range(2):
                    sp.wait_ge(x_loaded[h], 16 * b)
                    load_x(b, h)
            with sp.Fori(0, E) as e:
                for c in range(C):
                    sp.dma_start(wgu[:, e, c, 0:F], w_g[e, c * P:(c + 1) * P, :]).then_inc(experts_loaded, 16)
                    sp.dma_start(wgu[:, e, c, F:2 * F], w_u[e, c * P:(c + 1) * P, :]).then_inc(experts_loaded, 16)
                    sp.dma_start(wdn[:, e, c, :], w_d[e, c * P:(c + 1) * P, :]).then_inc(experts_loaded, 16)

            for b in range(B):
                for h in range(2):
                    n = 6 * b + 3 * h
                    cols = slice(h * HALF, (h + 1) * HALF)
                    for m in range(2):
                        sp.wait_ge(lo_ready, n + m + 1)
                        q_rows = q_hl[b, 8 * m:8 * m + 8, :, cols].rearrange("n (s d) q -> s n d q", s=2)
                        sp.dma_start(q_rows[0], rope_hi[m][:, :].bitcast(F32)).then_inc(qk_stored[m], 16)
                        sp.dma_start(q_rows[1], rope_lo[m][:, :].bitcast(F32)).then_inc(qk_stored[m], 16)
                    sp.wait_ge(lo_ready, n + 3)
                    for j, part in enumerate((rope_hi, rope_hi, rope_lo, rope_lo)):
                        sp.dma_start(k_st[b, :, HD * j:HD * (j + 1), cols],
                                     part[2][0:KV * HD, :].bitcast(F32)).then_inc(qk_stored[2], 16)

            def load_q(dst, done, g, h):
                b, kv = g // KV, g % KV
                src = q_hl[b].rearrange("(r k) d q -> k d r q", k=KV)[kv][:, :, h * HALF:(h + 1) * HALF]
                for j in range(2):
                    sp.dma_start(dst[h][2 * HD * j:2 * HD * (j + 1), :, :].bitcast(F32), src).then_inc(done[h], 16)

            def load_k(dst, done, g, p):
                sp.dma_start(dst[p][0:STACK, :].bitcast(F32), k_st[g // KV, g % KV]).then_inc(done[p], 16)

            def load_m(h):
                for row, part in ((STACK, m_hi), (STACK + 1, m_lo)):
                    sp.dma_start(qb[h][row:row + 1, :, :].rearrange("o r (t c) -> o (r t) c", c=P).bitcast(F32),
                                 part[h][:, :].bitcast(F32)).then_inc(qb_loaded[h], 16)

            for m in range(3):
                sp.wait_ge(qk_stored[m], (32, 32, 64)[m] * 2 * B)
            load_k(ka, ka_loaded, 0, 0)
            for h in range(2):
                load_q(qa, qa_loaded, 0, h)
            load_k(ka, ka_loaded, 1, 1)
            load_k(kb, kb_loaded, 0, 0)
            for h in range(2):
                load_q(qb, qb_loaded, 0, h)
                sp.wait_ge(mx_scored, uses_before(h + 1))
                load_q(qa, qa_loaded, 1, h)
                if h == 0:
                    sp.wait_ge(mx_taken, uses_before(1) + TURN + 1)
                    load_m(0)

            def load_rows(t, i):
                sp.dma_start(rows[i][:, :], rows_in[bass.ts(t, P), :]).then_inc(rows_loaded[i], 16)

            sp.wait_ge(scattered, 16 * 2 * NT)
            for i in range(4):
                load_rows(i, i)
            with sp.Fori(0, SLOTS // 4 - 1) as j:
                for i in range(4):
                    sp.wait_ge(xt_ready, 4 * j + i + 1)
                    load_rows(4 * j + i + 4, i)

            def period(g, p, last):
                if not last:
                    load_k(ka, ka_loaded, g + 2, p)
                sp.wait_ge(st_ready, 2 * KT * 2 * g + 1)
                load_k(kb, kb_loaded, g + 1, 1 - p)
                for h in range(2):
                    u = 2 * g + h
                    sp.wait_ge(mx_taken, uses_before(u + 2) + TURN + 1)
                    load_m(1 - h)
                    sp.wait_ge(st_ready, 2 * KT * (u + 1))
                    load_q(qb, qb_loaded, g + 1, h)
                    if not last:
                        sp.wait_ge(mx_scored, uses_before(u + 3))
                        load_q(qa, qa_loaded, g + 2, h)

            with sp.Fori(0, G // 2 - 1) as j:
                for p in range(2):
                    period(2 * j + p, p, False)
            period(G - 2, 0, True)
            sp.wait_ge(mx_taken, uses_before(2 * G) + 1)
            load_m(1)

            def store(t, i):
                sp.wait_ge(fin_ready, t + 1)
                sp.dma_start(out_t[:, t, :], fin[i][:, :]).then_inc(stored[i], 16)

            with sp.Fori(0, NT // 2) as j:
                for i in range(2):
                    store(2 * j + i, i)
            for i in range(2):
                sp.wait_ge(stored[i], 16 * NT // 2)

        @block.gpsimd
        def _(pool):
            pool.memset(zeros[:, :], 0.0).then_inc(pool_made, 1)
            pool.memset(ident[:, :], 0.0).then_inc(pool_made, 1)
            pool.memset(earlier[:, :], 1.0).then_inc(pool_made, 1)
            pool.memset(ones[:, :], 1.0).then_inc(pool_made, 1)
            pool.memset(wo_s[:, :, :], 0.0).then_inc(pool_made, 1)
            pool.wait_ge(pool_made, 5)
            pool.affine_select(out=ident[:, :], in_=ident[:, :], compare_op=ALU.not_equal, fill=1.0,
                               base=0, pattern=[[-1, P]], channel_multiplier=1).then_inc(pool_made, 1)
            pool.affine_select(out=earlier[:, :], in_=earlier[:, :], compare_op=ALU.is_gt, fill=0.0,
                               base=0, pattern=[[1, P]], channel_multiplier=-1).then_inc(pool_made, 1)
            pool.memset(eps[:, :], LN_EPS).then_inc(pool_made, 1)
            pool.iota(expert_no[:, :, :], pattern=[[0, 2 * NT], [1, E]], base=0, channel_multiplier=0,
                      allow_small_or_imprecise_dtypes=True).then_inc(pool_made, 1)
            pool.iota(limit[:, :, :], pattern=[[0, E], [P, NT]], base=0, channel_multiplier=0,
                      allow_small_or_imprecise_dtypes=True).then_inc(pool_made, 1)
            pool.iota(slot_no[:, :, :], pattern=[[1, SLOTS], [0, E]], base=0, channel_multiplier=0,
                      allow_small_or_imprecise_dtypes=True).then_inc(pool_made, 1)
            for p in range(2):
                pool.memset(v_st[p][:, :, HD + 1:], 0.0).then_inc(pool_made, 1)
                pool.memset(v_st[p][:, :, HD:HD + 1], 1.0).then_inc(pool_made, 1)
            pool.wait_ge(pool_made, 15)
            for n, q in enumerate(qa + qb):
                pool.memset(q[STACK:P, :, :].bitcast(F32), 0.0).then_inc(stacks_padded, 1)
                pool.wait_ge(stacks_padded, n + 1)
            pool.sem_inc(o_t_free, 2)

            for b in range(B):
                for h in range(2):
                    k = 2 * b + h
                    for m in range(3):
                        rows_m = (P, P, KV * HD)[m]
                        pool.wait_ge(swapped, 3 * k + m + 1)
                        pool.tensor_tensor(rope_b[m][0:rows_m, :], rope_b[m][0:rows_m, :],
                                           sin_s[0:rows_m, h * HALF:(h + 1) * HALF], ALU.mult).then_inc(sin_done, 1)

            pool.wait_ge(places_ready, 1)
            pool.wait_ge(rows_zeroed, 16)
            for n in range(2 * NT):
                pool.indirect_dma_start(
                    out=rows_in[:, :], out_offset=bass.IndirectOffsetOnAxis(ap=place_i[:, n:n + 1], axis=0),
                    in_=xn[:, n % NT, :], in_offset=None).then_inc(scattered, 16)

            def store_rows(t, i):
                pool.wait_ge(y_copied, t + 1)
                pool.dma_start(rows_out[bass.ts(t, P), :], y_s[i]).then_inc(y_stored[i], 16)

            with pool.Fori(0, SLOTS // 4) as j:
                for i in range(4):
                    store_rows(4 * j + i, i)

            def stage_v(g, p):
                pool.tensor_copy(v_st[p][:, :, 0:HD],
                                 v_all[:, (g // KV) * ST_T:(g // KV + 1) * ST_T, (g % KV) * HD:(g % KV + 1) * HD]).then_inc(v_staged, 1)

            pool.wait_ge(vr_taken, 4 * B)
            stage_v(0, 0)
            stage_v(1, 1)

            pool.wait_ge(gates_ready, 1)
            for i in range(4):
                pool.wait_ge(y_stored[i], 16 * SLOTS // 4)

            def mix_tile(t):
                for k in range(2):
                    pool.indirect_dma_start(
                        out=y_got[k][:, :], out_offset=None, in_=rows_out[:, :],
                        in_offset=bass.IndirectOffsetOnAxis(ap=place_i[:, k * NT + t:k * NT + t + 1], axis=0)
                    ).then_inc(y_gathered, 16)
                pool.wait_ge(y_gathered, 32 * (t + 1))
                for k in range(2):
                    pool.tensor_scalar(y_got[k][:, :], y_got[k][:, :], gate[:, k, t:t + 1], None,
                                       ALU.mult).then_inc(mix, 1)
                pool.wait_ge(mix, 4 * t + 2)
                pool.tensor_tensor(y_got[0][:, :], y_got[0][:, :], y_got[1][:, :], ALU.add).then_inc(mix, 1)
                pool.wait_ge(mix, 4 * t + 3)
                pool.tensor_tensor(xs[:, t, :], xs[:, t, :], y_got[0][:, :], ALU.add).then_inc(mix, 1)
                pool.wait_ge(mix, 4 * t + 4)

            for u in range(2 * G):
                pool.wait_ge(rden_ready, u + 1)
                pool.tensor_tensor(o_n.rearrange("p (n d) -> p n d", d=32), o_q.rearrange("p (n d) -> p n d", d=32),
                                   rden[:, :].unsqueeze(2).to_broadcast([P, HALF // 32, 32]), ALU.mult).then_inc(divided, 1)
                mix_tile(u)
                pool.wait_ge(attn_ready, u + 1)
                g, q0 = u // 2, (u // 2 // KV) * S + (u % 2) * HALF
                pool.tensor_copy(attn_t[:, g % KV, q0:q0 + HALF], o_t[u % 2]).then_inc(o_t_free, 1)
                if u % 2 and g < G - 2:
                    pool.wait_ge(products_done, 2 * KT * (g + 1))
                    stage_v(g + 2, g % 2)

        @block.scalar
        def _(act):
            for c in range(C):
                rows_c = slice(c * P, (c + 1) * P)
                act.dma_start(wqk[:, c, 0:NH * HD], w_q[rows_c, :]).then_inc(small_loaded, 16)
                act.dma_start(wqk[:, c, NH * HD:], w_k[rows_c, :]).then_inc(small_loaded, 16)
                act.dma_start(wvr[:, c, 0:KV * HD], w_v[rows_c, :]).then_inc(small_loaded, 16)
                act.dma_start(wvr[:, c, KV * HD:], w_r[rows_c, :]).then_inc(small_loaded, 16)
            act.dma_start(cos_s[:, :], cos_t).then_inc(small_loaded, 16)
            act.dma_start(sin_s[:, :], sin_t).then_inc(small_loaded, 16)
            act.wait_ge(pool_made, 8)
            for r in range(R):
                act.dma_start(wo_s[32 * r:32 * r + HD, :, :],
                              w_o.rearrange("(r k d) n -> r d k n", r=R, d=HD)[r]).then_inc(wo_loaded, 16)
            act.dma_start(rows_in.rearrange("(t p) d -> p t d", p=P),
                          zeros[:, :].unsqueeze(1).to_broadcast([P, SLOTS, D])).then_inc(rows_zeroed, 16)

            def copy_columns(k):
                for c in range(C):
                    act.wait_ge(tr_ready, C * k + c + 1)
                    if k >= 2:
                        act.wait_ge(pj_ready, 3 * (k - 1))
                    act.activation(xn_t[k % 2][:, c, :], tr_ps[c], ACT.Copy).then_inc(xn_t_ready, 1)

            for k in range(2 * B):
                act.wait_ge(stats_ready, k + 1)
                act.activation(std[k % 2][:, :], mean_var[k % 2][:, :, 1], ACT.Sqrt, bias=eps[:, 0:1]).then_inc(std_ready, 1)
                if k == 1:
                    copy_columns(0)
            for k in range(2 * B):
                if k < 2 * B - 1:
                    copy_columns(k + 1)
                for m in range(3):
                    rows_m = (P, P, KV * HD)[m]
                    act.wait_ge(pj_ready, 3 * k + m + 1)
                    act.wait_ge(lo_ready, 3 * (k - 1) + m + 1 if k else 0)
                    act.activation(rope_a[m][0:rows_m, :], pj_ps[m][0:rows_m, :], ACT.Copy).then_inc(pj_taken, 1)
                for m in range(3):
                    rows_m = (P, P, KV * HD)[m]
                    act.wait_ge(rope_done, 3 * k + m + 1)
                    act.wait_ge(qk_stored[m], (32, 32, 64)[m] * k)
                    act.activation(rope_hi[m][0:rows_m, :], rope_a[m][0:rows_m, :], ACT.Copy).then_inc(hi_ready, 1)

            act.wait_ge(diff_ready, 1)
            act.activation(gate_t[:, 1, :], gate_t[:, 0, :], ACT.Exp).then_inc(gate_exp, 1)

            def expert(t, i, first=False, last=False):
                act.wait_ge(gu_ready, t + 1)
                act.activation(act_g[i], gu_ps[i][:, 0:F], ACT.Silu).then_inc(silu_ready, 1)
                if not first:
                    act.wait_ge(ht_ready, t)
                    act.activation(act_t[1 - i].rearrange("p c n -> p (c n)"), ht_ps[1 - i][:, 0:F],
                                   ACT.Copy).then_inc(act_t_ready, 1)
                if not last:
                    act.wait_ge(xt_ready, t + 2)
                    act.activation(rows_t[1 - i].rearrange("p c n -> p (c n)"), xt_ps[1 - i][:, 0:D],
                                   ACT.Copy).then_inc(rows_t_ready, 1)

            act.wait_ge(xt_ready, 1)
            act.activation(rows_t[0].rearrange("p c n -> p (c n)"), xt_ps[0][:, 0:D],
                           ACT.Copy).then_inc(rows_t_ready, 1)
            expert(0, 0, first=True)
            expert(1, 1)
            with act.Fori(1, SLOTS // 2 - 1) as j:
                for i in range(2):
                    expert(2 * j + i, i)
            expert(SLOTS - 2, 0)
            expert(SLOTS - 1, 1, last=True)
            act.wait_ge(ht_ready, SLOTS)
            act.activation(act_t[1].rearrange("p c n -> p (c n)"), ht_ps[1][:, 0:F],
                           ACT.Copy).then_inc(act_t_ready, 1)

            def exps(u, first=False):
                for kt in range(KT):
                    s = KT * u + kt
                    if not first or kt >= 2:
                        act.wait_ge(products_done, s - 1)
                    for j in range(2):
                        act.wait_ge(st_ready, 2 * s + j + 1)
                        act.activation(probs[kt % 2][:, 2 * j:2 * j + 2, :].rearrange("p r q -> p (r q)"),
                                       st_ps[j][:, :], ACT.Exp, scale=1.0 / math.sqrt(HD)).then_inc(exp_done, 1)

            exps(0, True)
            with act.Fori(1, 2 * G) as u:
                exps(u)

            act.wait_ge(o_t_free, 2 * G + 2)
            def copy_attn(j, first=False):
                for i in range(2):
                    t = 2 * j + i
                    if not first:
                        act.wait_ge(wo_ready, t - 1)
                    act.activation(attn_c[i][:, :, :], attn_t[:, :, bass.ts(t, P)], ACT.Copy).then_inc(attn_copied, 1)

            copy_attn(0, True)
            with act.Fori(1, NT // 2) as j:
                copy_attn(j)

        @block.vector
        def _(dve):
            dve.sem_inc(o_free, 1)
            for p in range(2):
                nc.vector.memset(kb[p][STACK:P, :].bitcast(F32), 0.0).then_inc(vec_made, 1)
                nc.vector.memset(ka[p][STACK:P, :].bitcast(F32), 0.0).then_inc(vec_made, 1)
            dve.wait_ge(vec_made, 4)
            for p in range(2):
                nc.vector.memset(kb[p][STACK:AUG, :].bitcast(F32), 1.0).then_inc(vec_made, 1)
            for b in range(B):
                for h in range(2):
                    k = 2 * b + h
                    t0 = b * ST_T + h * TB
                    N_LN = 2
                    dve.wait_ge(x_loaded[h], 16 * (b + 1))
                    for j in range(TB):
                        last = nc.vector.bn_stats(stats[h][:, j, :], xs[:, t0 + j, :])
                    last.then_inc(dve_ln, 1)
                    dve.wait_ge(dve_ln, N_LN * k + 1)
                    for j in range(TB):
                        last = nc.vector.bn_aggr(mean_var[h][:, j, :], stats[h][:, j, :])
                    last.then_inc(stats_ready, 1)
                    dve.wait_ge(std_ready, k + 1)
                    nc.vector.reciprocal(rstd[h][:, :], std[h][:, :]).then_inc(dve_ln, 1)
                    dve.wait_ge(dve_ln, N_LN * k + 2)
                    dve.wait_ge(stats_ready, k + 1)
                    for j in range(TB):
                        last = nc.vector.tensor_scalar(xn[:, t0 + j, :], xs[:, t0 + j, :], mean_var[h][:, j, 0:1],
                                                       rstd[h][:, j:j + 1], ALU.subtract, ALU.mult)
                    last.then_inc(xn_ready, 1)
            for b in range(B):
                for h in range(2):
                    k = 2 * b + h
                    t0 = b * ST_T + h * TB
                    dve.wait_ge(vr_ready, k + 1)
                    vr = vr_ps[:, 0:TB * (KV * HD + E)].rearrange("p (t n) -> p t n", t=TB)
                    nc.vector.tensor_copy(v_all[:, bass.ds(t0, TB), :], vr[:, :, 0:KV * HD]).then_inc(vr_taken, 1)
                    nc.vector.tensor_copy(logits[:, bass.ds(t0, TB), :], vr[:, :, KV * HD:]).then_inc(vr_taken, 1)
                    for m in range(3):
                        rows_m = (P, P, KV * HD)[m]
                        dve.wait_ge(pj_taken, 3 * k + m + 1)
                        dve.wait_ge(small_loaded, 16 * (4 * C + 2))
                        nc.vector.stream_shuffle(rope_b[m][0:rows_m, :], rope_a[m][0:rows_m, :],
                                                 [d ^ 1 for d in range(32)]).then_inc(swapped, 1)
                    for m in range(3):
                        rows_m = (P, P, KV * HD)[m]
                        dve.wait_ge(swapped, 3 * k + m + 1)
                        nc.vector.tensor_tensor(rope_a[m][0:rows_m, :], rope_a[m][0:rows_m, :],
                                                cos_s[0:rows_m, h * HALF:(h + 1) * HALF], ALU.mult).then_inc(cos_done, 1)
                    for m in range(3):
                        rows_m = (P, P, KV * HD)[m]
                        dve.wait_ge(cos_done, 3 * k + m + 1)
                        dve.wait_ge(sin_done, 3 * k + m + 1)
                        nc.vector.tensor_tensor(rope_a[m][0:rows_m, :], rope_a[m][0:rows_m, :],
                                                rope_b[m][0:rows_m, :], ALU.add).then_inc(rope_done, 1)
                    for m in range(3):
                        rows_m = (P, P, KV * HD)[m]
                        dve.wait_ge(hi_ready, 3 * k + m + 1)
                        dve.wait_ge(rope_done, 3 * k + m + 1)
                        nc.vector.tensor_tensor(rope_lo[m][0:rows_m, :], rope_a[m][0:rows_m, :],
                                                rope_hi[m][0:rows_m, :].bitcast(F32), ALU.subtract).then_inc(lo_ready, 1)

            n_route = [0]

            def link(ins):
                ins.then_inc(route, 1)
                n_route[0] += 1
                dve.wait_ge(route, n_route[0])

            dve.wait_ge(pool_made, 11)
            dve.wait_ge(vr_taken, 4 * B)
            numbers = expert_no[:, 0:NT, :]

            def pick(lg, k):
                link(nc.vector.tensor_reduce(top[:, k, :], lg[:, :, :], X_AXIS, ALU.max))
                link(nc.vector.tensor_tensor(cand[:, :, :], lg[:, :, :],
                                             top[:, k, :].unsqueeze(2).to_broadcast([P, NT, E]), ALU.is_ge))
                link(nc.vector.scalar_tensor_tensor(cand[:, :, :], cand[:, :, :], -float(E), numbers,
                                                    ALU.mult, ALU.add))
                link(nc.vector.tensor_reduce(choice[:, k, :], cand[:, :, :], X_AXIS, ALU.min))
                link(nc.vector.tensor_scalar(choice[:, k, :], choice[:, k, :], float(E), None, ALU.add))
                link(nc.vector.tensor_tensor(onehot[:, k, :, :], numbers,
                                             choice[:, k, :].unsqueeze(2).to_broadcast([P, NT, E]), ALU.is_equal))

            pick(logits, 0)
            link(nc.vector.scalar_tensor_tensor(logits2[:, :, :], onehot[:, 0, :, :], -FAR, logits[:, :, :],
                                                ALU.mult, ALU.add))
            pick(logits2, 1)
            nc.vector.engine_nop().then_inc(choices_ready, 1)
            nc.vector.tensor_tensor(gate_t[:, 0, :], top[:, 1, :], top[:, 0, :], ALU.subtract).then_inc(diff_ready, 1)

            flat = "p t e -> p (t e)"
            dve.wait_ge(counts_ready, 1)
            link(nc.vector.tensor_copy(totals[:, :, :].rearrange(flat), total_ps[:, 0:2 * NT * E]))
            link(nc.vector.tensor_copy(sums[0][:, :, :].rearrange(flat), total_ps[:, 0:2 * NT * E]))
            src, step = 0, 1
            while step < 2 * NT:
                a, z = sums[src], sums[1 - src]
                nc.vector.tensor_copy(z[:, 0:step, :], a[:, 0:step, :])
                link(nc.vector.tensor_tensor(z[:, step:, :], a[:, step:, :], a[:, 0:2 * NT - step, :], ALU.add))
                src, step = 1 - src, 2 * step
            incl = sums[src]
            link(nc.vector.tensor_tensor(over[:, :, :], incl[:, 2 * NT - 1, :].unsqueeze(2).to_broadcast([P, E, NT]),
                                         limit[:, :, :], ALU.is_gt))
            link(nc.vector.reduce_sum(n_tiles[:, :], over[:, :, :], axis=X_AXIS))
            link(nc.vector.tensor_copy(cum[0][:, :], n_tiles[:, :]))
            csrc, step = 0, 1
            while step < E:
                a, z = cum[csrc], cum[1 - csrc]
                nc.vector.tensor_copy(z[:, 0:step], a[:, 0:step])
                link(nc.vector.tensor_tensor(z[:, step:], a[:, step:], a[:, 0:E - step], ALU.add))
                csrc, step = 1 - csrc, 2 * step
            ends = cum[csrc]
            link(nc.vector.tensor_tensor(slot_ge[:, :, :], ends[:, :].unsqueeze(1).to_broadcast([P, SLOTS, E]),
                                         slot_no[:, :, :], ALU.is_le))
            link(nc.vector.reduce_sum(slot_e[:, :], slot_ge[:, :, :], axis=X_AXIS))
            link(nc.vector.tensor_scalar(slot_ei[:, :], slot_e[:, :], float(E - 1), None, ALU.min))
            link(nc.vector.tensor_tensor(n_tiles[:, :], ends[:, :], n_tiles[:, :], ALU.subtract))
            link(nc.vector.tensor_scalar(n_tiles[:, :], n_tiles[:, :], float(P), None, ALU.mult))
            link(nc.vector.tensor_tensor(totals[:, :, :], incl[:, :, :], totals[:, :, :], ALU.subtract))
            link(nc.vector.tensor_tensor(totals[:, :, :].rearrange(flat), totals[:, :, :].rearrange(flat),
                                         rank_ps[:, 0:2 * NT * E], ALU.add))
            link(nc.vector.tensor_tensor(totals[:, :, :], totals[:, :, :],
                                         n_tiles[:, :].unsqueeze(1).to_broadcast([P, 2 * NT, E]), ALU.add))
            link(nc.vector.tensor_tensor(totals[:, :, :].rearrange(flat), totals[:, :, :].rearrange(flat),
                                         onehot[:, :, :, :].rearrange("p k t e -> p (k t e)"), ALU.mult))
            link(nc.vector.reduce_sum(place[:, :], totals[:, :, :], axis=X_AXIS))
            nc.vector.tensor_copy(place_i[:, :], place[:, :]).then_inc(places_ready, 1)
            dve.wait_ge(gate_exp, 1)
            link(nc.vector.tensor_scalar(gate_t[:, 2, :], gate_t[:, 1, :], 1.0, None, ALU.add))
            link(nc.vector.reciprocal(gate[:, 0, :], gate_t[:, 2, :]))
            nc.vector.tensor_tensor(gate[:, 1, :], gate_t[:, 1, :], gate[:, 0, :], ALU.mult).then_inc(gates_ready, 1)

            def unit_max(h, a, n):
                i = a + (a >= TURN)
                dve.wait_ge(mx_scored, n + i + 1)
                nc.vector.reduce_max(mx[h][:, a // 2, a % 2:a % 2 + 1], mx_ps[i % 3], axis=X_AXIS).then_inc(mx_taken, 1)

            def join_maxima(h, uses):
                dve.wait_ge(mx_taken, uses)
                nc.vector.tensor_reduce(neg_mx[:, :], mx[h][:, :, :], X_AXIS, ALU.max, negate=True).then_inc(neg_mx_ready, 1)

            def split_maxima(v, h, n, i, sent):
                dve.wait_ge(mx_scored, n + i + 1)
                if sent is not None:
                    dve.wait_ge(qb_loaded[h], sent)
                turned = mx_ps[TURN % 3][0:R * QT, 0:P]
                nc.vector.tensor_copy(m_hi[h][:, :], turned).then_inc(m_hi_ready, 1)
                dve.wait_ge(m_hi_ready, v + 1)
                nc.vector.tensor_tensor(m_lo[h][:, :], turned, m_hi[h][:, :].bitcast(F32), ALU.subtract).then_inc(mx_taken, 1)

            for a in range(NA):
                dve.wait_ge(mx_scored, a + 1)
                nc.vector.reduce_max(mx[0][:, a // 2, a % 2:a % 2 + 1], mx_ps[(a + (a >= TURN)) % 3],
                                     axis=X_AXIS).then_inc(mx_taken, 1)
            join_maxima(0, NA)
            for a in range(NA):
                if a == TURN:
                    split_maxima(0, 0, uses_before(1), TURN, None)
                unit_max(1, a, uses_before(1))
            join_maxima(1, uses_before(2))

            def expert(t, i):
                dve.wait_ge(silu_ready, t + 1)
                nc.vector.tensor_scalar(act_g[i], act_g[i], CLAMP, -CLAMP, ALU.min, ALU.max).then_inc(clip_done, 1)
                dve.wait_ge(clip_done, t + 1)
                nc.vector.tensor_tensor(act_h[i], gu_ps[i][:, F:2 * F], act_g[i], ALU.mult).then_inc(act_ready, 1)

            def take_y(t, q, i, stores):
                dve.wait_ge(y_ready, t + 1)
                if stores is not None:
                    dve.wait_ge(y_stored[q], stores)
                nc.vector.tensor_copy(y_s[q], y_ps[i][:, 0:D]).then_inc(y_copied, 1)

            for t in range(4):
                expert(t, t % 2)
                if t >= 2:
                    take_y(t - 2, t - 2, t % 2, None)
            for t in range(4, 8):
                expert(t, t % 2)
                take_y(t - 2, (t - 2) % 4, t % 2, None if t < 6 else 16)
            with dve.Fori(2, SLOTS // 4) as j:
                for i in range(4):
                    expert(4 * j + i, i % 2)
                    take_y(4 * j + i - 2, (i + 2) % 4, i % 2, 16 * (j - 1 if i < 2 else j))
            for t in range(SLOTS - 2, SLOTS):
                take_y(t, t % 4, t % 2, 16 * (SLOTS // 4 - 1))

            def turn_output(u):
                dve.wait_ge(products_done, KT * (u + 1))
                nc.vector.transpose(o_q, o_ps).then_inc(o_free, 1)
                dve.wait_ge(o_free, u + 2)
                nc.vector.reciprocal(rden[:, :], o_q.rearrange("p (n d) -> p n d", d=32)[:, :, HD]).then_inc(rden_ready, 1)

            def turn_back(u, h):
                dve.wait_ge(divided, u + 1)
                dve.wait_ge(o_t_free, u + 1)
                nc.vector.transpose(o_t[h], o_n).then_inc(attn_ready, 1)

            def group(g, first=False):
                for h in range(2):
                    u = 2 * g + h
                    n = uses_before(u + 2)
                    for a in range(NA):
                        if a == TURN:
                            split_maxima(u + 1, 1 - h, n, TURN, None if first and h == 0 else 64 * (g + h))
                        if a == NA - 8 and not (first and h == 0):
                            turn_back(u - 1, 1 - h)
                        unit_max(h, a, n)
                    join_maxima(h, n + NI)
                    turn_output(u)

            group(0, first=True)
            with dve.Fori(1, G - 1) as g:
                group(g)
            u = 2 * G - 2
            split_maxima(u + 1, 1, uses_before(u + 2), 0, 64 * (G - 1))
            turn_back(u - 1, 1)
            turn_output(u)
            turn_back(u, 0)
            turn_output(u + 1)
            turn_back(u + 1, 1)

            dve.wait_ge(mix, 4 * NT)
            def finish(j, first=False):
                for i in range(2):
                    t = 2 * j + i
                    dve.wait_ge(wo_ready, t + 1)
                    if not first:
                        dve.wait_ge(stored[i], 16 * j)
                    nc.vector.tensor_tensor(fin[i][:, :], wo_ps[i][:, 0:D], xs[:, t, :], ALU.add).then_inc(fin_ready, 1)

            finish(0, True)
            with dve.Fori(1, NT // 2) as j:
                finish(j)

        @block.tensor
        def _(pe):
            mm = nc.tensor.matmul
            pe.wait_ge(pool_made, 7)

            def columns(k):
                pe.wait_ge(xn_ready, k + 1)
                for c in range(C):
                    if k:
                        pe.wait_ge(xn_t_ready, C * (k - 1) + c + 1)
                    for j in range(TB):
                        last = nc.tensor.transpose(tr_ps[c][:, j * P:(j + 1) * P],
                                                   xn[:, k * TB + j, c * P:(c + 1) * P], ident[:, :])
                    last.then_inc(tr_ready, 1)

            NV = KV * HD + E
            columns(0)
            pe.wait_ge(small_loaded, 16 * (4 * C + 2))
            for k in range(2 * B):
                h = k % 2
                if k < 2 * B - 1:
                    columns(k + 1)
                pe.wait_ge(xn_t_ready, C * (k + 1))
                pe.wait_ge(vr_taken, 2 * k)
                for j in range(TB):
                    for c in range(C):
                        last = mm(vr_ps[:, j * NV:(j + 1) * NV], xn_t[h][:, c, j * P:(j + 1) * P], wvr[:, c, :],
                                  start=(c == 0), stop=(c == C - 1))
                last.then_inc(vr_ready, 1)
                for m in range(3):
                    rows_m = (P, P, KV * HD)[m]
                    pe.wait_ge(pj_taken, 3 * (k - 1) + m + 1 if k else 0)
                    for c in range(C):
                        last = mm(pj_ps[m][0:rows_m, :], wqk[:, c, m * P:m * P + rows_m], xn_t[h][:, c, :],
                                  start=(c == 0), stop=(c == C - 1))
                    last.then_inc(pj_ready, 1)

            pe.wait_ge(choices_ready, 1)
            hot = onehot[:, :, :, :].rearrange("p k t e -> p (k t e)")
            mm(rank_ps[:, 0:2 * NT * E], earlier[:, :], hot, start=True, stop=True)
            mm(total_ps[:, 0:2 * NT * E], ones[:, :], hot, start=True, stop=True).then_inc(counts_ready, 1)

            def score_max(h, p, a, i, taken):
                r, qt, kh = a // (2 * QT), a // 2 % QT, a % 2
                if taken is not None:
                    pe.wait_ge(mx_taken, taken)
                mm(mx_ps[i % 3], qa[h][:, r, qt * P:(qt + 1) * P], ka[p][:, kh * HALF:(kh + 1) * HALF],
                   start=True, stop=True).then_inc(mx_scored, 1)

            def turn_maxima(v, taken):
                pe.wait_ge(neg_mx_ready, v + 1)
                pe.wait_ge(mx_taken, taken)
                nc.tensor.transpose(mx_ps[TURN % 3][0:R * QT, 0:P], neg_mx[:, :], ident[:, :]).then_inc(mx_scored, 1)

            pe.wait_ge(vec_made, 6)
            pe.wait_ge(stacks_padded, 4)
            pe.wait_ge(ka_loaded[0], 16)
            pe.wait_ge(qa_loaded[0], 32)
            for a in range(NA):
                score_max(0, 0, a, a + (a >= TURN), a - 1 if a >= 2 else None)
            pe.wait_ge(qa_loaded[1], 32)
            for a in range(NA):
                n = uses_before(1)
                if a == TURN:
                    turn_maxima(0, n + TURN - 2)
                i = a + (a >= TURN)
                score_max(1, 0, a, i, n + i - 2)

            expert_reg = [pe.alloc_register(f"expert{i}") for i in range(4)]

            def load_expert(t, i):
                pe.reg_load(expert_reg[i], slot_ei[0:1, bass.ds(t, 1)])

            def expert_of(i):
                return pe.snap(expert_reg[i], min_val=0, max_val=E - 1)

            def to_columns(t, i):
                for c in range(C):
                    last = nc.tensor.transpose(xt_ps[i % 2][:, c * P:(c + 1) * P], rows[i][:, c * P:(c + 1) * P], ident[:, :])
                last.then_inc(xt_ready, 1)

            def gate_up(t, i):
                e = expert_of(i)
                pe.wait_ge(rows_t_ready, t + 1)
                for c in range(C):
                    last = mm(gu_ps[i % 2][:, :], rows_t[i % 2][:, c, :], wgu[:, e, c, :], start=(c == 0), stop=(c == C - 1))
                last.then_inc(gu_ready, 1)

            def act_columns(t, i):
                pe.wait_ge(act_ready, t + 1)
                for c in range(C):
                    last = nc.tensor.transpose(ht_ps[i % 2][:, c * P:(c + 1) * P], act_h[i % 2][:, c * P:(c + 1) * P], ident[:, :])
                last.then_inc(ht_ready, 1)

            def down(t, i, reused):
                e = expert_of(i)
                if reused:
                    pe.wait_ge(y_copied, t - 1)
                pe.wait_ge(act_t_ready, t + 1)
                for c in range(C):
                    last = mm(y_ps[i % 2][:, 0:D], act_t[i % 2][:, c, :], wdn[:, e, c, :], start=(c == 0), stop=(c == C - 1))
                last.then_inc(y_ready, 1)

            def expert(t, i, loads, first=False, last=False):
                gate_up(t, i)
                if not last:
                    load_expert(t + 1, (i + 1) % 4)
                if not first:
                    act_columns(t - 1, i - 1)
                if not last:
                    pe.wait_ge(rows_loaded[(i + 1) % 4], loads)
                    to_columns(t + 1, (i + 1) % 4)
                if not isinstance(t, int) or t >= 2:
                    down(t - 2, (i - 2) % 4, not isinstance(t, int) or t >= 4)

            pe.wait_ge(places_ready, 1)
            load_expert(0, 0)
            pe.wait_ge(experts_loaded, 16 * 3 * C * E)
            pe.wait_ge(rows_loaded[0], 16)
            to_columns(0, 0)
            for t in range(8):
                expert(t, t % 4, 16 * ((t + 1) // 4 + 1), first=t == 0)
            with pe.Fori(2, SLOTS // 4 - 1) as j:
                for i in range(4):
                    expert(4 * j + i, i, 16 * (j + 1 + (i + 1) // 4))
            for t in range(SLOTS - 4, SLOTS):
                expert(t, t % 4, 16 * ((t + 1) // 4 + 1), last=t == SLOTS - 1)
            act_columns(SLOTS - 1, 3)
            for t in range(SLOTS - 2, SLOTS):
                down(t, t % 4, True)

            def scores(h, p, kt, s, j):
                if s is not None:
                    pe.wait_ge(exp_done, 2 * (s - 1) + j + 1)
                for r in (2 * j, 2 * j + 1):
                    last = mm(st_ps[j][:, (r - 2 * j) * HALF:(r - 2 * j + 1) * HALF],
                              kb[p][:, kt * P:(kt + 1) * P], qb[h][:, r, :], start=True, stop=True)
                last.then_inc(st_ready, 1)

            def values(p, kt, s, u):
                pe.wait_ge(exp_done, 2 * (s + 1))
                if kt == 0:
                    pe.wait_ge(o_free, u + 1)
                for r in range(R):
                    last = mm(o_ps[32 * r:32 * (r + 1), :], v_st[p][:, kt, :], probs[kt % 2][:, r, :],
                              start=(kt == 0), stop=(kt == KT - 1))
                last.then_inc(products_done, 1)

            pe.wait_ge(y_copied, SLOTS)
            pe.wait_ge(kb_loaded[0], 16)
            pe.wait_ge(qb_loaded[0], 64)
            for j in range(2):
                scores(0, 0, 0, None, j)

            def group(g, p, last):
                for h in range(2):
                    u = 2 * g + h
                    n = uses_before(u + 2)

                    def maximum(a):
                        if not last:
                            if a == TURN:
                                turn_maxima(u + 1, n + TURN - 2)
                            i = a + (a >= TURN)
                            score_max(h, 1 - p, a, i, n + i - 2)

                    for kt in range(KT):
                        s = KT * u + kt
                        if not last and kt == 0:
                            pe.wait_ge(qa_loaded[h], 32 * (g + 2))
                            if h == 0:
                                pe.wait_ge(ka_loaded[1 - p], 16 * ((g - p) // 2 + p) + 16)
                        if last and h == 0 and kt == 0:
                            turn_maxima(u + 1, n)
                        if kt == KT - 1 and h == 0:
                            pe.wait_ge(qb_loaded[1], 64 * (g + 1))
                        if kt == KT - 1 and h == 1 and not last:
                            pe.wait_ge(kb_loaded[1 - p], 16 * ((g - p) // 2 + p) + 16)
                            pe.wait_ge(qb_loaded[0], 64 * (g + 2))
                        for j in range(2):
                            maximum(4 * kt + j)
                            if kt < KT - 1:
                                scores(h, p, kt + 1, s + 1, j)
                            elif h == 0:
                                scores(1, p, 0, s + 1, j)
                            elif not last:
                                scores(0, 1 - p, 0, s + 1, j)
                        maximum(4 * kt + 2)
                        if h == 0 and kt == 0:
                            pe.wait_ge(v_staged, g + 1)
                        values(p, kt, s, u)
                        maximum(4 * kt + 3)

            with pe.Fori(0, G // 2 - 1) as j:
                for p in range(2):
                    group(2 * j + p, p, False)
            group(G - 2, 0, False)
            group(G - 1, 1, True)

            pe.wait_ge(wo_loaded, 16 * R)
            def project(j, first=False):
                for i in range(2):
                    t = 2 * j + i
                    pe.wait_ge(attn_copied, t + 1)
                    if not first:
                        pe.wait_ge(fin_ready, t - 1)
                    for kv in range(KV):
                        last = mm(wo_ps[i][:, 0:D], attn_c[i][:, kv, :], wo_s[:, kv, :], start=(kv == 0), stop=(kv == KV - 1))
                    last.then_inc(wo_ready, 1)

            project(0, True)
            with pe.Fori(1, NT // 2) as j:
                project(j)


def rope_tables(seq):
    half = HD // 2
    freqs = (np.float32(1.0) / np.power(np.float32(10000.0), np.arange(half, dtype=np.float32) / np.float32(half))).astype(np.float32)
    angles = np.arange(seq, dtype=np.float32)[:, None] * freqs[None, :]
    dims = np.arange(P) % HD
    sign = np.where(dims % 2 == 0, -1.0, 1.0).astype(np.float32)
    cos_t = np.cos(angles)[:, dims // 2].T
    sin_t = np.sin(angles)[:, dims // 2].T * sign[:, None]
    return np.ascontiguousarray(cos_t, np.float32), np.ascontiguousarray(sin_t, np.float32)


NAMES = ["L0_attn_x", "L0_attn_W_q", "L0_attn_W_k", "L0_attn_W_v", "L0_attn_W_o",
         "L0_ffn_Wr", "L0_ffn_Wg", "L0_ffn_Wu", "L0_ffn_Wd"]


def kernel(**inputs):
    import concourse.bacc as bacc
    from concourse.bass_utils import run_bass_kernel_spmd

    nc = bacc.Bacc("TRN2", target_bir_lowering=False, num_devices=1)
    arrays = {f"in_{n}": np.ascontiguousarray(inputs[n]) for n in NAMES}
    seq = arrays["in_L0_attn_x"].shape[1]
    arrays["rope_cos"], arrays["rope_sin"] = rope_tables(seq)
    args = [nc.dram_tensor(n, a.shape, F32, kind="ExternalInput").ap() for n, a in arrays.items()]
    out = nc.dram_tensor("out", arrays["in_L0_attn_x"].shape, F32, kind="ExternalOutput").ap()
    build(nc, *args, out)
    r = run_bass_kernel_spmd(nc, [arrays], core_ids=[0])
    return r.results[0]["out"]
```

```python
import math
from contextlib import ExitStack

import numpy as np

import concourse.bass as bass
from concourse import mybir

F32 = mybir.dt.float32
F32R = mybir.dt.float32r
I32 = mybir.dt.int32
U32 = mybir.dt.uint32
ALU = mybir.AluOpType
ACT = mybir.ActivationFunctionType
X_AXIS = mybir.AxisListType.X

P = 128
HD = 16
LN_EPS = 1e-5
CLAMP = 7.0
FAR = 3.0e38


def build(nc, x, w_q, w_k, w_v, w_o, w_r, w_g, w_u, w_d, cos_t, sin_t, out):
    B, S, D = x.shape
    C = D // P
    NH = w_q.shape[1] // HD
    KV = w_k.shape[1] // HD
    R = NH // KV
    E, _, F = w_g.shape
    NT = B * S // P
    ST_T = S // P
    G = B * KV
    HALF = S // 2
    KT = S // P
    QT = HALF // P
    TB = 4
    STACK = 4 * HD
    AUG = STACK + 2
    SLOTS = 2 * NT + E
    NA = R * QT * 2
    TURN = 4
    NI = NA + 1
    assert C == 2 and R == 4 and KT == 8 and QT == 4 and E == 8 and HALF == 512 and F == 256
    assert B == 2 and TB * P == HALF

    xt = x.rearrange("b (t p) d -> p (b t) d", p=P)
    out_t = out.rearrange("b (t p) d -> p (b t) d", p=P)

    q_hl = nc.dram_tensor("q_hl", [B, NH, 2 * HD, S], F32, kind="Internal").ap()
    k_st = nc.dram_tensor("k_st", [B, KV, STACK, S], F32, kind="Internal").ap()
    rows_in = nc.dram_tensor("rows_in", [SLOTS * P, D], F32, kind="Internal").ap()
    rows_out = nc.dram_tensor("rows_out", [SLOTS * P, D], F32, kind="Internal").ap()

    with ExitStack() as ctx:
        def sb(name, shape, dt=F32):
            return ctx.enter_context(nc.sbuf_tensor(name, shape, dt))

        def sem(name):
            return ctx.enter_context(nc.semaphore(name))

        big = sb("big", [P, E * C * 3 * F])
        wgu = big[:, 0:E * C * 2 * F].rearrange("p (e c n) -> p e c n", e=E, c=C)
        wdn = big[:, E * C * 2 * F:].rearrange("p (e c n) -> p e c n", e=E, c=C)
        KC = KV // 2
        attn_t = big[:, 0:KC * B * S].rearrange("p (c t) -> p c t", c=KC)
        probs = [big[:, KC * B * S + i * R * HALF:KC * B * S + (i + 1) * R * HALF]
                 .rearrange("p (r q) -> p r q", r=R) for i in range(2)]
        xs = sb("xs", [P, NT, D])
        xn = sb("xn", [P, NT, D])
        xn_t = [sb(f"xn_t{k}", [P, C, HALF]) for k in range(2 * B)]
        wqk = sb("wqk", [P, C, (NH + KV) * HD])
        wvr = sb("wvr", [P, C, KV * HD + E])
        wo_s = sb("wo_s", [P, KV // 2, D])
        cos_s = sb("cos_s", [P, S])
        sin_s = sb("sin_s", [P, S])
        rope_a = [sb(f"rope_a{m}", [P, HALF]) for m in range(3)]
        rope_b = [sb(f"rope_b{m}", [P, HALF]) for m in range(3)]
        rope_hi = [sb(f"rope_hi{m}", [P, HALF], F32R) for m in range(3)]
        rope_lo = [sb(f"rope_lo{m}", [P, HALF], F32R) for m in range(3)]
        stats = [sb(f"stats{h}", [P, TB, 6]) for h in range(2)]
        mean_var = [sb(f"mean_var{h}", [P, TB, 2]) for h in range(2)]
        std = [sb(f"std{h}", [P, TB]) for h in range(2)]
        rstd = [sb(f"rstd{h}", [P, TB]) for h in range(2)]
        eps = sb("eps", [P, 1])
        v_all = sb("v_all", [P, NT, KV * HD])
        ident = sb("ident", [P, P])
        earlier = sb("earlier", [P, P])
        ones = sb("ones", [P, P])
        zeros = sb("zeros", [P, D])
        logits = sb("logits", [P, NT, E])
        logits2 = sb("logits2", [P, NT, E])
        expert_no = sb("expert_no", [P, 2 * NT, E])
        cand = sb("cand", [P, NT, E])
        top = sb("top", [P, 2, NT])
        choice = sb("choice", [P, 2, NT])
        onehot = sb("onehot", [P, 2, NT, E])
        gate = sb("gate", [P, 2, NT])
        gate_t = sb("gate_t", [P, 3, NT])
        sums = [sb(f"sums{i}", [P, 2 * NT, E]) for i in range(2)]
        totals = sb("totals", [P, 2 * NT, E])
        limit = sb("limit", [P, E, NT])
        over = sb("over", [P, E, NT])
        n_tiles = sb("n_tiles", [P, E])
        cum = [sb(f"cum{i}", [P, E]) for i in range(2)]
        slot_no = sb("slot_no", [P, SLOTS, E])
        slot_ge = sb("slot_ge", [P, SLOTS, E])
        slot_e = sb("slot_e", [P, SLOTS])
        slot_ei = sb("slot_ei", [P, SLOTS], I32)
        place = sb("place", [P, 2 * NT])
        place_i = sb("place_i", [P, 2 * NT], U32)
        spare = xn[:, :, :].rearrange("p t d -> p (t d)")

        def in_spare(n, width):
            return spare[:, n * width:(n + 1) * width]

        rows = [in_spare(i, D) for i in range(4)]
        rows_t = [in_spare(4 + i, D).rearrange("p (c n) -> p c n", c=C) for i in range(2)]
        act_g = [in_spare(6 + i, F) for i in range(2)]
        act_h = [in_spare(8 + i, F) for i in range(2)]
        act_t = [in_spare(10 + i, F).rearrange("p (c n) -> p c n", c=C) for i in range(2)]
        y_s = [in_spare(12 + i, D) for i in range(4)]
        o_q = in_spare(2, HALF)
        o_n = [in_spare(3 + h, HALF) for h in range(2)]
        o_t = [in_spare(h, HALF) for h in range(2)]
        qa = [sb(f"qa{h}", [P, R, HALF], F32R) for h in range(2)]
        qb = [sb(f"qb{h}", [P, R, HALF], F32R) for h in range(2)]
        ka = [sb(f"ka{p}", [P, S], F32R) for p in range(2)]
        kb = [sb(f"kb{p}", [P, S], F32R) for p in range(2)]
        v_st = [sb(f"v_st{p}", [P, KT, 32]) for p in range(2)]
        mx = [sb(f"mx{h}", [P, R * QT, 2]) for h in range(2)]
        neg_mx = sb("neg_mx", [P, R * QT])
        m_hi = [sb(f"m_hi{h}", [R * QT, P], F32R) for h in range(2)]
        m_lo = [sb(f"m_lo{h}", [R * QT, P], F32R) for h in range(2)]
        rden = sb("rden", [P, HALF // 32])
        y_got = [rope_a[0][:, k * D:(k + 1) * D] for k in range(2)]
        fin = [rope_a[1 + i // 2][:, i % 2 * D:(i % 2 + 1) * D] for i in range(4)]

        bank = [ctx.enter_context(nc.psum_tensor(f"bank{i}", [P, 1024], F32)) for i in range(4)]

        def half_bank(i):
            return bank[i // 2][:, 512 * (i % 2):512 * (i % 2) + 512]

        tr_ps = [half_bank(0), half_bank(1)]
        vr_ps = half_bank(2)
        pj_ps = [half_bank(3), half_bank(4), half_bank(5)]
        rank_ps = half_bank(6)
        total_ps = half_bank(7)
        xt_ps = [half_bank(0)[:, i * D:(i + 1) * D] for i in range(2)]
        ht_ps = [half_bank(1)[:, i * F:(i + 1) * F] for i in range(2)]
        gu_ps = [half_bank(2), half_bank(3)]
        y_ps = [half_bank(7)[:, i * D:(i + 1) * D] for i in range(2)]
        st_ps = [bank[0], bank[1]]
        mx_ps = [half_bank(4), half_bank(5), half_bank(6)]
        o_ps = half_bank(7)
        wo_ps = mx_ps

        def side(o, s):
            return o.rearrange("p (n d) -> p n d", d=32)[:, :, HD * s:HD * (s + 1)]

        x_loaded = [sem(f"x_loaded{k}") for k in range(4)]
        small_loaded = sem("small_loaded")
        wo_loaded = sem("wo_loaded")
        experts_loaded = sem("experts_loaded")
        rows_zeroed = sem("rows_zeroed")
        pool_made = sem("pool_made")
        vec_made = sem("vec_made")
        stacks_padded = sem("stacks_padded")
        dve_ln = sem("dve_ln")
        stats_ready = sem("stats_ready")
        std_ready = sem("std_ready")
        xn_ready = sem("xn_ready")
        tr_ready = sem("tr_ready")
        xn_t_ready = sem("xn_t_ready")
        vr_ready = sem("vr_ready")
        vr_taken = sem("vr_taken")
        pj_ready = sem("pj_ready")
        swapped = sem("swapped")
        cos_done = sem("cos_done")
        sin_done = sem("sin_done")
        rope_done = sem("rope_done")
        hi_ready = sem("hi_ready")
        lo_ready = sem("lo_ready")
        qk_stored = [sem(f"qk_stored{m}") for m in range(3)]
        route = sem("route")
        choices_ready = sem("choices_ready")
        counts_ready = sem("counts_ready")
        diff_ready = sem("diff_ready")
        gate_exp = sem("gate_exp")
        gates_ready = sem("gates_ready")
        places_ready = sem("places_ready")
        scattered = sem("scattered")
        rows_loaded = [sem(f"rows_loaded{i}") for i in range(4)]
        xt_ready = sem("xt_ready")
        rows_t_ready = sem("rows_t_ready")
        gu_ready = sem("gu_ready")
        silu_ready = sem("silu_ready")
        clip_done = sem("clip_done")
        act_ready = sem("act_ready")
        ht_ready = sem("ht_ready")
        act_t_ready = sem("act_t_ready")
        y_ready = sem("y_ready")
        y_copied = sem("y_copied")
        y_stored = [sem(f"y_stored{i}") for i in range(4)]
        qa_loaded = [sem(f"qa_loaded{h}") for h in range(2)]
        qb_loaded = [sem(f"qb_loaded{h}") for h in range(2)]
        ka_loaded = [sem(f"ka_loaded{p}") for p in range(2)]
        kb_loaded = [sem(f"kb_loaded{p}") for p in range(2)]
        v_staged = sem("v_staged")
        mx_scored = sem("mx_scored")
        mx_taken = sem("mx_taken")
        neg_mx_ready = sem("neg_mx_ready")
        m_hi_ready = sem("m_hi_ready")
        st_ready = sem("st_ready")
        exp_done = sem("exp_done")
        products_done = sem("products_done")
        o_free = sem("o_free")
        rden_ready = sem("rden_ready")
        divided = sem("divided")
        attn_ready = sem("attn_ready")
        o_t_free = sem("o_t_free")
        y_gathered = sem("y_gathered")
        mix = sem("mix")
        mixed = sem("mixed")
        wo_ready = sem("wo_ready")
        fin_ready = sem("fin_ready")
        stored = [sem(f"stored{i}") for i in range(4)]

        SHARED = 16

        def shared_with(t):
            n = t - (SLOTS - SHARED)
            return list(range(2 * NA * n // SHARED, 2 * NA * (n + 1) // SHARED))

        def out_tiles(n):
            return (range(0, KT), range(KT, KT + QT), range(KT + QT, NT))[n]

        def uses_before(v):
            return NI * v - 1

        block = ctx.enter_context(nc.Block())

        @block.sync
        def _(sp):
            for k in range(2 * B):
                sp.dma_start(xs[:, k * TB:(k + 1) * TB, :], xt[:, k * TB:(k + 1) * TB, :]).then_inc(x_loaded[k], 16)
            wo_rows = w_o.rearrange("(r c s d) n -> r s d c n", r=R, s=2, d=HD)
            for r in range(R):
                for s in range(2):
                    sp.dma_start(wo_s[32 * r + HD * s:32 * r + HD * (s + 1), :, :], wo_rows[r, s]).then_inc(wo_loaded, 16)
            sp.wait_ge(pool_made, 7)
            sp.dma_start(rows_in.rearrange("(t p) d -> p t d", p=P),
                         zeros[:, :].unsqueeze(1).to_broadcast([P, SLOTS, D])).then_inc(rows_zeroed, 16)
            with sp.Fori(0, E) as e:
                for c in range(C):
                    sp.dma_start(wgu[:, e, c, 0:F], w_g[e, c * P:(c + 1) * P, :]).then_inc(experts_loaded, 16)
                    sp.dma_start(wgu[:, e, c, F:2 * F], w_u[e, c * P:(c + 1) * P, :]).then_inc(experts_loaded, 16)
                    sp.dma_start(wdn[:, e, c, :], w_d[e, c * P:(c + 1) * P, :]).then_inc(experts_loaded, 16)

            for b in range(B):
                for h in range(2):
                    n = 6 * b + 3 * h
                    cols = slice(h * HALF, (h + 1) * HALF)
                    for m in range(2):
                        sp.wait_ge(lo_ready, n + m + 1)
                        q_rows = q_hl[b, 8 * m:8 * m + 8, :, cols].rearrange("n (s d) q -> s n d q", s=2)
                        sp.dma_start(q_rows[0], rope_hi[m][:, :].bitcast(F32)).then_inc(qk_stored[m], 16)
                        sp.dma_start(q_rows[1], rope_lo[m][:, :].bitcast(F32)).then_inc(qk_stored[m], 16)
                    sp.wait_ge(lo_ready, n + 3)
                    for j, part in enumerate((rope_hi, rope_hi, rope_lo, rope_lo)):
                        sp.dma_start(k_st[b, :, HD * j:HD * (j + 1), cols],
                                     part[2][0:KV * HD, :].bitcast(F32)).then_inc(qk_stored[2], 16)

            def load_q(dst, done, g, h):
                b, kv = g // KV, g % KV
                src = q_hl[b].rearrange("(r k) d q -> k d r q", k=KV)[kv][:, :, h * HALF:(h + 1) * HALF]
                for j in range(2):
                    sp.dma_start(dst[h][2 * HD * j:2 * HD * (j + 1), :, :].bitcast(F32), src).then_inc(done[h], 16)

            def load_k(dst, done, g, p):
                sp.dma_start(dst[p][0:STACK, :].bitcast(F32), k_st[g // KV, g % KV]).then_inc(done[p], 16)

            def load_m(h):
                for row, part in ((STACK, m_hi), (STACK + 1, m_lo)):
                    sp.dma_start(qb[h][row:row + 1, :, :].rearrange("o r (t c) -> o (r t) c", c=P).bitcast(F32),
                                 part[h][:, :].bitcast(F32)).then_inc(qb_loaded[h], 16)


            def load_rows(t, i):
                sp.dma_start(rows[i][:, :], rows_in[bass.ts(t, P), :]).then_inc(rows_loaded[i], 16)

            sp.wait_ge(scattered, 16 * 2 * NT)
            for i in range(4):
                load_rows(i, i)
            for m in range(3):
                sp.wait_ge(qk_stored[m], (32, 32, 64)[m] * 2 * B)
            load_k(ka, ka_loaded, 0, 0)
            for h in range(2):
                load_q(qa, qa_loaded, 0, h)
            load_k(ka, ka_loaded, 1, 1)
            load_k(kb, kb_loaded, 0, 0)
            for h in range(2):
                load_q(qb, qb_loaded, 0, h)
            with sp.Fori(0, SLOTS // 4 - 1) as j:
                for i in range(4):
                    sp.wait_ge(xt_ready, 4 * j + i + 1)
                    load_rows(4 * j + i + 4, i)
            for h in range(2):
                sp.wait_ge(mx_scored, uses_before(h + 1))
                load_q(qa, qa_loaded, 1, h)
                if h == 0:
                    sp.wait_ge(mx_taken, uses_before(1) + TURN + 1)
                    load_m(0)

            def period(g, p, last):
                if not last:
                    load_k(ka, ka_loaded, g + 2, p)
                sp.wait_ge(st_ready, 2 * KT * 2 * g + 1)
                load_k(kb, kb_loaded, g + 1, 1 - p)
                for h in range(2):
                    u = 2 * g + h
                    sp.wait_ge(mx_taken, uses_before(u + 2) + TURN + 1)
                    load_m(1 - h)
                    sp.wait_ge(st_ready, 2 * KT * (u + 1))
                    load_q(qb, qb_loaded, g + 1, h)
                    if not last:
                        sp.wait_ge(mx_scored, uses_before(u + 3))
                        load_q(qa, qa_loaded, g + 2, h)

            with sp.Fori(0, G // 2 - 1) as j:
                for p in range(2):
                    period(2 * j + p, p, False)
            period(G - 2, 0, True)
            sp.wait_ge(mx_taken, uses_before(2 * G) + 1)
            load_m(1)

            for t in range(NT):
                sp.wait_ge(fin_ready, t + 1)
                sp.dma_start(out_t[:, t, :], fin[t % 4]).then_inc(stored[t % 4], 16)
            for i in range(4):
                sp.wait_ge(stored[i], 16 * NT // 4)

        @block.gpsimd
        def _(pool):
            pool.memset(zeros[:, :], 0.0).then_inc(pool_made, 1)
            pool.memset(ident[:, :], 0.0).then_inc(pool_made, 1)
            pool.memset(earlier[:, :], 1.0).then_inc(pool_made, 1)
            pool.memset(ones[:, :], 1.0).then_inc(pool_made, 1)
            pool.wait_ge(pool_made, 4)
            pool.affine_select(out=ident[:, :], in_=ident[:, :], compare_op=ALU.not_equal, fill=1.0,
                               base=0, pattern=[[-1, P]], channel_multiplier=1).then_inc(pool_made, 1)
            pool.affine_select(out=earlier[:, :], in_=earlier[:, :], compare_op=ALU.is_gt, fill=0.0,
                               base=0, pattern=[[1, P]], channel_multiplier=-1).then_inc(pool_made, 1)
            pool.memset(eps[:, :], LN_EPS).then_inc(pool_made, 1)
            pool.iota(expert_no[:, :, :], pattern=[[0, 2 * NT], [1, E]], base=0, channel_multiplier=0,
                      allow_small_or_imprecise_dtypes=True).then_inc(pool_made, 1)
            pool.iota(limit[:, :, :], pattern=[[0, E], [P, NT]], base=0, channel_multiplier=0,
                      allow_small_or_imprecise_dtypes=True).then_inc(pool_made, 1)
            pool.iota(slot_no[:, :, :], pattern=[[1, SLOTS], [0, E]], base=0, channel_multiplier=0,
                      allow_small_or_imprecise_dtypes=True).then_inc(pool_made, 1)
            for p in range(2):
                pool.memset(v_st[p][:, :, HD + 1:], 0.0).then_inc(pool_made, 1)
                pool.memset(v_st[p][:, :, HD:HD + 1], 1.0).then_inc(pool_made, 1)
            pool.wait_ge(pool_made, 14)
            for n, q in enumerate(qa + qb):
                pool.memset(q[STACK:P, :, :].bitcast(F32), 0.0).then_inc(stacks_padded, 1)
                pool.wait_ge(stacks_padded, n + 1)
            pool.sem_inc(o_t_free, 2)

            pool.wait_ge(places_ready, 1)
            pool.wait_ge(rows_zeroed, 16)
            for n in range(2 * NT):
                pool.indirect_dma_start(
                    out=rows_in[:, :], out_offset=bass.IndirectOffsetOnAxis(ap=place_i[:, n:n + 1], axis=0),
                    in_=xn[:, n % NT, :], in_offset=None).then_inc(scattered, 16)

            def store_rows(t, i):
                pool.wait_ge(y_copied, t + 1)
                pool.dma_start(rows_out[bass.ts(t, P), :], y_s[i]).then_inc(y_stored[i], 16)

            with pool.Fori(0, SLOTS // 4) as j:
                for i in range(4):
                    store_rows(4 * j + i, i)

            def stage_v(g, p):
                pool.tensor_copy(v_st[p][:, :, 0:HD],
                                 v_all[:, (g // KV) * ST_T:(g // KV + 1) * ST_T, (g % KV) * HD:(g % KV + 1) * HD]).then_inc(v_staged, 1)

            pool.wait_ge(vr_taken, 4 * B)
            stage_v(0, 0)
            stage_v(1, 1)

            pool.wait_ge(gates_ready, 1)
            for i in range(4):
                pool.wait_ge(y_stored[i], 16 * SLOTS // 4)

            def mix_tile(t):
                for k in range(2):
                    pool.indirect_dma_start(
                        out=y_got[k][:, :], out_offset=None, in_=rows_out[:, :],
                        in_offset=bass.IndirectOffsetOnAxis(ap=place_i[:, k * NT + t:k * NT + t + 1], axis=0)
                    ).then_inc(y_gathered, 16)
                pool.wait_ge(y_gathered, 32 * (t + 1))
                for k in range(2):
                    pool.tensor_scalar(y_got[k][:, :], y_got[k][:, :], gate[:, k, t:t + 1], None,
                                       ALU.mult).then_inc(mix, 1)
                pool.wait_ge(mix, 4 * t + 2)
                pool.tensor_tensor(y_got[0][:, :], y_got[0][:, :], y_got[1][:, :], ALU.add).then_inc(mix, 1)
                pool.wait_ge(mix, 4 * t + 3)
                pool.tensor_tensor(xs[:, t, :], xs[:, t, :], y_got[0][:, :], ALU.add).then_inc(mix, 1)
                pool.wait_ge(mix, 4 * t + 4)

            MIX_UNITS = 12
            for u in range(2 * G - 1):
                g, h = u // 2, u % 2
                pool.wait_ge(rden_ready, u + 1)
                if g % 2 == 0 and g:
                    pool.wait_ge(attn_ready, g - 1 + h)
                pool.tensor_tensor(side(o_n[h], g % 2), side(o_q, 0),
                                   rden[:, :].unsqueeze(2).to_broadcast([P, HALF // 32, HD]), ALU.mult).then_inc(divided, 1)
                if u < MIX_UNITS:
                    for t in range(u * NT // MIX_UNITS, (u + 1) * NT // MIX_UNITS):
                        mix_tile(t)
                if g % 2 and g < G - 1:
                    pool.wait_ge(attn_ready, g + h)
                    q0 = g // KV * S + h * HALF
                    pool.tensor_copy(attn_t[:, g % KV // 2, q0:q0 + HALF], o_t[h]).then_inc(o_t_free, 1)
                if h and g < G - 2:
                    pool.wait_ge(products_done, 2 * KT * (g + 1))
                    stage_v(g + 2, g % 2)

        @block.scalar
        def _(act):
            def by_chunk(w):
                return w.rearrange("(c p) n -> p c n", p=P)

            act.dma_start(wvr[:, :, 0:KV * HD], by_chunk(w_v)).then_inc(small_loaded, 16)
            act.dma_start(wvr[:, :, KV * HD:], by_chunk(w_r)).then_inc(small_loaded, 16)
            act.dma_start(wqk[:, :, 0:NH * HD], by_chunk(w_q)).then_inc(small_loaded, 16)
            act.dma_start(wqk[:, :, NH * HD:], by_chunk(w_k)).then_inc(small_loaded, 16)
            act.dma_start(cos_s[:, :], cos_t).then_inc(small_loaded, 16)
            act.dma_start(sin_s[:, :], sin_t).then_inc(small_loaded, 16)

            def copy_columns(k):
                for c in range(C):
                    act.wait_ge(tr_ready, C * k + c + 1)
                    act.activation(xn_t[k][:, c, :], tr_ps[c], ACT.Copy).then_inc(xn_t_ready, 1)

            act.wait_ge(pool_made, 7)
            for k in range(2 * B):
                act.wait_ge(stats_ready, k + 1)
                act.activation(std[k % 2][:, :], mean_var[k % 2][:, :, 1], ACT.Sqrt, bias=eps[:, 0:1]).then_inc(std_ready, 1)
                if k:
                    copy_columns(k - 1)
            copy_columns(2 * B - 1)
            act.wait_ge(diff_ready, 1)
            act.activation(gate_t[:, 1, :], gate_t[:, 0, :], ACT.Exp).then_inc(gate_exp, 1)
            for k in range(2 * B):
                for m in range(3):
                    rows_m = (P, P, KV * HD)[m]
                    act.wait_ge(rope_done, 3 * k + m + 1)
                    act.wait_ge(qk_stored[m], (32, 32, 64)[m] * k)
                    act.activation(rope_hi[m][0:rows_m, :], rope_a[m][0:rows_m, :], ACT.Copy).then_inc(hi_ready, 1)

            def expert(t, i, first=False, last=False):
                act.wait_ge(gu_ready, t + 1)
                act.activation(act_g[i], gu_ps[i][:, 0:F], ACT.Silu).then_inc(silu_ready, 1)
                if not first:
                    act.wait_ge(ht_ready, t)
                    act.activation(act_t[1 - i].rearrange("p c n -> p (c n)"), ht_ps[1 - i],
                                   ACT.Copy).then_inc(act_t_ready, 1)
                if not last:
                    act.wait_ge(xt_ready, t + 2)
                    act.activation(rows_t[1 - i].rearrange("p c n -> p (c n)"), xt_ps[1 - i],
                                   ACT.Copy).then_inc(rows_t_ready, 1)

            act.wait_ge(xt_ready, 1)
            act.activation(rows_t[0].rearrange("p c n -> p (c n)"), xt_ps[0],
                           ACT.Copy).then_inc(rows_t_ready, 1)
            expert(0, 0, first=True)
            expert(1, 1)
            with act.Fori(1, SLOTS // 2 - 1) as j:
                for i in range(2):
                    expert(2 * j + i, i)
            expert(SLOTS - 2, 0)
            expert(SLOTS - 1, 1, last=True)
            act.wait_ge(ht_ready, SLOTS)
            act.activation(act_t[1].rearrange("p c n -> p (c n)"), ht_ps[1],
                           ACT.Copy).then_inc(act_t_ready, 1)

            def exps(u, first=False):
                for kt in range(KT):
                    s = KT * u + kt
                    if not first or kt >= 2:
                        act.wait_ge(products_done, s - 1)
                    for j in range(2):
                        act.wait_ge(st_ready, 2 * s + j + 1)
                        act.activation(probs[kt % 2][:, 2 * j:2 * j + 2, :].rearrange("p r q -> p (r q)"),
                                       st_ps[j][:, :], ACT.Exp, scale=1.0 / math.sqrt(HD)).then_inc(exp_done, 1)

            exps(0, True)
            with act.Fori(1, 2 * G) as u:
                exps(u)

        @block.vector
        def _(dve):
            dve.sem_inc(o_free, 1)
            for b in range(B):
                for h in range(2):
                    k = 2 * b + h
                    t0 = b * ST_T + h * TB
                    N_LN = 2
                    dve.wait_ge(x_loaded[k], 16)
                    for j in range(TB):
                        last = nc.vector.bn_stats(stats[h][:, j, :], xs[:, t0 + j, :])
                    last.then_inc(dve_ln, 1)
                    dve.wait_ge(dve_ln, N_LN * k + 1)
                    for j in range(TB):
                        last = nc.vector.bn_aggr(mean_var[h][:, j, :], stats[h][:, j, :])
                    last.then_inc(stats_ready, 1)
                    dve.wait_ge(std_ready, k + 1)
                    nc.vector.reciprocal(rstd[h][:, :], std[h][:, :]).then_inc(dve_ln, 1)
                    dve.wait_ge(dve_ln, N_LN * k + 2)
                    dve.wait_ge(stats_ready, k + 1)
                    for j in range(TB):
                        last = nc.vector.tensor_scalar(xn[:, t0 + j, :], xs[:, t0 + j, :], mean_var[h][:, j, 0:1],
                                                       rstd[h][:, j:j + 1], ALU.subtract, ALU.mult)
                    last.then_inc(xn_ready, 1)
            for b in range(B):
                for h in range(2):
                    k = 2 * b + h
                    t0 = b * ST_T + h * TB
                    dve.wait_ge(vr_ready, k + 1)
                    vr = vr_ps[:, 0:TB * (KV * HD + E)].rearrange("p (t n) -> p t n", t=TB)
                    nc.vector.tensor_copy(v_all[:, t0:t0 + TB, :], vr[:, :, 0:KV * HD]).then_inc(vr_taken, 1)
                    nc.vector.tensor_copy(logits[:, t0:t0 + TB, :], vr[:, :, KV * HD:]).then_inc(vr_taken, 1)

            n_route = [0]

            def link(ins):
                ins.then_inc(route, 1)
                n_route[0] += 1
                dve.wait_ge(route, n_route[0])

            dve.wait_ge(pool_made, 10)
            dve.wait_ge(vr_taken, 4 * B)
            numbers = expert_no[:, 0:NT, :]

            def pick(lg, k):
                link(nc.vector.tensor_reduce(top[:, k, :], lg[:, :, :], X_AXIS, ALU.max))
                link(nc.vector.tensor_tensor(cand[:, :, :], lg[:, :, :],
                                             top[:, k, :].unsqueeze(2).to_broadcast([P, NT, E]), ALU.is_ge))
                link(nc.vector.scalar_tensor_tensor(cand[:, :, :], cand[:, :, :], -float(E), numbers,
                                                    ALU.mult, ALU.add))
                link(nc.vector.tensor_reduce(choice[:, k, :], cand[:, :, :], X_AXIS, ALU.min))
                link(nc.vector.tensor_scalar(choice[:, k, :], choice[:, k, :], float(E), None, ALU.add))
                link(nc.vector.tensor_tensor(onehot[:, k, :, :], numbers,
                                             choice[:, k, :].unsqueeze(2).to_broadcast([P, NT, E]), ALU.is_equal))

            pick(logits, 0)
            link(nc.vector.scalar_tensor_tensor(logits2[:, :, :], onehot[:, 0, :, :], -FAR, logits[:, :, :],
                                                ALU.mult, ALU.add))
            pick(logits2, 1)
            nc.vector.engine_nop().then_inc(choices_ready, 1)
            nc.vector.tensor_tensor(gate_t[:, 0, :], top[:, 1, :], top[:, 0, :], ALU.subtract).then_inc(diff_ready, 1)

            flat = "p t e -> p (t e)"
            dve.wait_ge(counts_ready, 1)
            link(nc.vector.tensor_copy(totals[:, :, :].rearrange(flat), total_ps[:, 0:2 * NT * E]))
            link(nc.vector.tensor_copy(sums[0][:, :, :].rearrange(flat), total_ps[:, 0:2 * NT * E]))
            src, step = 0, 1
            while step < 2 * NT:
                a, z = sums[src], sums[1 - src]
                nc.vector.tensor_copy(z[:, 0:step, :], a[:, 0:step, :])
                link(nc.vector.tensor_tensor(z[:, step:, :], a[:, step:, :], a[:, 0:2 * NT - step, :], ALU.add))
                src, step = 1 - src, 2 * step
            incl = sums[src]
            link(nc.vector.tensor_tensor(over[:, :, :], incl[:, 2 * NT - 1, :].unsqueeze(2).to_broadcast([P, E, NT]),
                                         limit[:, :, :], ALU.is_gt))
            link(nc.vector.reduce_sum(n_tiles[:, :], over[:, :, :], axis=X_AXIS))
            link(nc.vector.tensor_copy(cum[0][:, :], n_tiles[:, :]))
            csrc, step = 0, 1
            while step < E:
                a, z = cum[csrc], cum[1 - csrc]
                nc.vector.tensor_copy(z[:, 0:step], a[:, 0:step])
                link(nc.vector.tensor_tensor(z[:, step:], a[:, step:], a[:, 0:E - step], ALU.add))
                csrc, step = 1 - csrc, 2 * step
            ends = cum[csrc]
            link(nc.vector.tensor_tensor(slot_ge[:, :, :], ends[:, :].unsqueeze(1).to_broadcast([P, SLOTS, E]),
                                         slot_no[:, :, :], ALU.is_le))
            link(nc.vector.reduce_sum(slot_e[:, :], slot_ge[:, :, :], axis=X_AXIS))
            link(nc.vector.tensor_scalar(slot_ei[:, :], slot_e[:, :], float(E - 1), None, ALU.min))
            link(nc.vector.tensor_tensor(n_tiles[:, :], ends[:, :], n_tiles[:, :], ALU.subtract))
            link(nc.vector.tensor_scalar(n_tiles[:, :], n_tiles[:, :], float(P), None, ALU.mult))
            link(nc.vector.tensor_tensor(totals[:, :, :], incl[:, :, :], totals[:, :, :], ALU.subtract))
            link(nc.vector.tensor_tensor(totals[:, :, :].rearrange(flat), totals[:, :, :].rearrange(flat),
                                         rank_ps[:, 0:2 * NT * E], ALU.add))
            link(nc.vector.tensor_tensor(totals[:, :, :], totals[:, :, :],
                                         n_tiles[:, :].unsqueeze(1).to_broadcast([P, 2 * NT, E]), ALU.add))
            link(nc.vector.tensor_tensor(totals[:, :, :].rearrange(flat), totals[:, :, :].rearrange(flat),
                                         onehot[:, :, :, :].rearrange("p k t e -> p (k t e)"), ALU.mult))
            link(nc.vector.reduce_sum(place[:, :], totals[:, :, :], axis=X_AXIS))
            nc.vector.tensor_copy(place_i[:, :], place[:, :]).then_inc(places_ready, 1)
            for p in range(2):
                nc.vector.memset(kb[p][STACK:P, :].bitcast(F32), 0.0).then_inc(vec_made, 1)
                nc.vector.memset(ka[p][STACK:P, :].bitcast(F32), 0.0).then_inc(vec_made, 1)
            dve.wait_ge(vec_made, 4)
            for p in range(2):
                nc.vector.memset(kb[p][STACK:AUG, :].bitcast(F32), 1.0).then_inc(vec_made, 1)
            dve.wait_ge(gate_exp, 1)
            link(nc.vector.tensor_scalar(gate_t[:, 2, :], gate_t[:, 1, :], 1.0, None, ALU.add))
            link(nc.vector.reciprocal(gate[:, 0, :], gate_t[:, 2, :]))
            nc.vector.tensor_tensor(gate[:, 1, :], gate_t[:, 1, :], gate[:, 0, :], ALU.mult).then_inc(gates_ready, 1)

            dve.wait_ge(small_loaded, 16 * 6)
            for k in range(2 * B):
                h = k % 2
                for m in range(3):
                    rows_m = (P, P, KV * HD)[m]
                    dve.wait_ge(pj_ready, 3 * k + m + 1)
                    nc.vector.stream_shuffle(rope_b[m][0:rows_m, :], pj_ps[m][0:rows_m, :],
                                             [d ^ 1 for d in range(32)]).then_inc(swapped, 1)
                    if k:
                        dve.wait_ge(hi_ready, 3 * (k - 1) + m + 1)
                        dve.wait_ge(lo_ready, 3 * (k - 1) + m + 1)
                    nc.vector.tensor_tensor(rope_a[m][0:rows_m, :], pj_ps[m][0:rows_m, :],
                                            cos_s[0:rows_m, h * HALF:(h + 1) * HALF], ALU.mult).then_inc(cos_done, 1)
                for m in range(3):
                    rows_m = (P, P, KV * HD)[m]
                    dve.wait_ge(swapped, 3 * k + m + 1)
                    nc.vector.tensor_tensor(rope_b[m][0:rows_m, :], rope_b[m][0:rows_m, :],
                                            sin_s[0:rows_m, h * HALF:(h + 1) * HALF], ALU.mult).then_inc(sin_done, 1)
                for m in range(3):
                    rows_m = (P, P, KV * HD)[m]
                    dve.wait_ge(cos_done, 3 * k + m + 1)
                    dve.wait_ge(sin_done, 3 * k + m + 1)
                    nc.vector.tensor_tensor(rope_a[m][0:rows_m, :], rope_a[m][0:rows_m, :],
                                            rope_b[m][0:rows_m, :], ALU.add).then_inc(rope_done, 1)
                for m in range(3):
                    rows_m = (P, P, KV * HD)[m]
                    dve.wait_ge(hi_ready, 3 * k + m + 1)
                    dve.wait_ge(rope_done, 3 * k + m + 1)
                    dve.wait_ge(qk_stored[m], (32, 32, 64)[m] * k)
                    nc.vector.tensor_tensor(rope_lo[m][0:rows_m, :], rope_a[m][0:rows_m, :],
                                            rope_hi[m][0:rows_m, :].bitcast(F32), ALU.subtract).then_inc(lo_ready, 1)

            def unit_max(h, a, n):
                i = a + (a >= TURN)
                dve.wait_ge(mx_scored, n + i + 1)
                nc.vector.reduce_max(mx[h][:, a // 2, a % 2:a % 2 + 1], mx_ps[i % 3], axis=X_AXIS).then_inc(mx_taken, 1)

            def join_maxima(h, uses):
                dve.wait_ge(mx_taken, uses)
                nc.vector.tensor_reduce(neg_mx[:, :], mx[h][:, :, :], X_AXIS, ALU.max, negate=True).then_inc(neg_mx_ready, 1)

            def split_maxima(v, h, n, i, sent):
                dve.wait_ge(mx_scored, n + i + 1)
                if sent is not None:
                    dve.wait_ge(qb_loaded[h], sent)
                turned = mx_ps[TURN % 3][0:R * QT, 0:P]
                nc.vector.tensor_copy(m_hi[h][:, :], turned).then_inc(m_hi_ready, 1)
                dve.wait_ge(m_hi_ready, v + 1)
                nc.vector.tensor_tensor(m_lo[h][:, :], turned, m_hi[h][:, :].bitcast(F32), ALU.subtract).then_inc(mx_taken, 1)

            def first_max(n):
                v, a = n // NA, n % NA
                if v:
                    if a == TURN:
                        split_maxima(0, 0, uses_before(1), TURN, None)
                    unit_max(1, a, uses_before(1))
                else:
                    dve.wait_ge(mx_scored, a + 1)
                    nc.vector.reduce_max(mx[0][:, a // 2, a % 2:a % 2 + 1], mx_ps[(a + (a >= TURN)) % 3],
                                         axis=X_AXIS).then_inc(mx_taken, 1)
                if a == NA - 1:
                    join_maxima(v, uses_before(1 + v))

            def expert(t, i):
                dve.wait_ge(silu_ready, t + 1)
                nc.vector.tensor_scalar(act_g[i], act_g[i], CLAMP, -CLAMP, ALU.min, ALU.max).then_inc(clip_done, 1)
                dve.wait_ge(clip_done, t + 1)
                nc.vector.tensor_tensor(act_h[i], gu_ps[i][:, F:2 * F], act_g[i], ALU.mult).then_inc(act_ready, 1)

            def take_y(t, q, i, stores):
                dve.wait_ge(y_ready, t + 1)
                if stores is not None:
                    dve.wait_ge(y_stored[q], stores)
                nc.vector.tensor_copy(y_s[q], y_ps[i]).then_inc(y_copied, 1)

            for t in range(4):
                expert(t, t % 2)
                if t >= 2:
                    take_y(t - 2, t - 2, t % 2, None)
            for t in range(4, 8):
                expert(t, t % 2)
                take_y(t - 2, (t - 2) % 4, t % 2, None if t < 6 else 16)
            with dve.Fori(2, (SLOTS - SHARED) // 4) as j:
                for i in range(4):
                    expert(4 * j + i, i % 2)
                    take_y(4 * j + i - 2, (i + 2) % 4, i % 2, 16 * (j - 1 if i < 2 else j))
            for t in range(SLOTS - SHARED, SLOTS):
                todo = shared_with(t)
                first_max(todo[0])
                expert(t, t % 2)
                for n in todo[1:3]:
                    first_max(n)
                take_y(t - 2, (t - 2) % 4, t % 2, 16 * ((t - 2) // 4))
                for n in todo[3:]:
                    first_max(n)
            for t in range(SLOTS - 2, SLOTS):
                take_y(t, t % 4, t % 2, 16 * (SLOTS // 4 - 1))

            def turn_output(u, first=False):
                dve.wait_ge(products_done, KT * (u + 1))
                if not first:
                    dve.wait_ge(divided, u)
                nc.vector.transpose(o_q, o_ps).then_inc(o_free, 1)

            def invert_sums(u):
                dve.wait_ge(o_free, u + 2)
                nc.vector.reciprocal(rden[:, :], o_q.rearrange("p (n d) -> p n d", d=32)[:, :, HD]).then_inc(rden_ready, 1)

            def turn_back(g, h):
                dve.wait_ge(divided, 2 * g + h + 1)
                dve.wait_ge(o_t_free, g + h)
                nc.vector.transpose(o_t[h], o_n[h]).then_inc(attn_ready, 1)

            def group(g, p, first=False):
                for h in range(2):
                    u = 2 * g + h
                    n = uses_before(u + 2)
                    for a in range(NA):
                        if a == 1 and not (first and h == 0):
                            join_maxima(1 - h, n)
                        if a == 2 and not (first and h == 0):
                            invert_sums(u - 1)
                        if a == TURN:
                            split_maxima(u + 1, 1 - h, n, TURN, None if first and h == 0 else 64 * (g + h))
                        if a == NA - 8 and p == h and not (first and h == 0):
                            turn_back(g - 1 + h, 1 - h)
                        unit_max(h, a, n)
                    turn_output(u, first and h == 0)

            group(0, 0, first=True)
            group(1, 1)
            with dve.Fori(1, G // 2 - 1) as j:
                for p in range(2):
                    group(2 * j + p, p)
            group(G - 2, 0)
            u = 2 * G - 2
            join_maxima(1, uses_before(u + 2))
            invert_sums(u - 1)
            split_maxima(u + 1, 1, uses_before(u + 2), 0, 64 * (G - 1))

            def finish(n):
                for t in out_tiles(n):
                    dve.wait_ge(wo_ready, t + 1)
                    if t >= 4:
                        dve.wait_ge(stored[t % 4], 16 * (t // 4))
                    nc.vector.tensor_tensor(fin[t % 4], wo_ps[t % 3][:, 0:D], xs[:, t, :], ALU.add).then_inc(fin_ready, 1)

            dve.wait_ge(mix, 4 * NT)
            finish(0)
            turn_output(u)
            invert_sums(u)
            dve.wait_ge(divided, u + 1)
            nc.vector.transpose(attn_t[:, KC - 1, (B - 1) * S:(B - 1) * S + HALF], o_n[0]).then_inc(attn_ready, 1)
            finish(1)
            turn_output(u + 1)
            invert_sums(u + 1)
            dve.wait_ge(rden_ready, u + 2)
            nc.vector.tensor_tensor(side(o_n[1], 1), side(o_q, 0),
                                    rden[:, :].unsqueeze(2).to_broadcast([P, HALF // 32, HD]), ALU.mult).then_inc(divided, 1)
            dve.wait_ge(divided, u + 2)
            nc.vector.transpose(attn_t[:, KC - 1, (B - 1) * S + HALF:B * S], o_n[1]).then_inc(attn_ready, 1)
            finish(2)

        @block.tensor
        def _(pe):
            mm = nc.tensor.matmul
            pe.wait_ge(pool_made, 6)

            def columns(k):
                pe.wait_ge(xn_ready, k + 1)
                for c in range(C):
                    if k:
                        pe.wait_ge(xn_t_ready, C * (k - 1) + c + 1)
                    for j in range(TB):
                        last = nc.tensor.transpose(tr_ps[c][:, j * P:(j + 1) * P],
                                                   xn[:, k * TB + j, c * P:(c + 1) * P], ident[:, :])
                    last.then_inc(tr_ready, 1)

            NV = KV * HD + E
            columns(0)
            pe.wait_ge(small_loaded, 16 * 6)
            for k in range(2 * B):
                if k < 2 * B - 1:
                    columns(k + 1)
                pe.wait_ge(xn_t_ready, C * (k + 1))
                pe.wait_ge(vr_taken, 2 * k)
                for j in range(TB):
                    for c in range(C):
                        last = mm(vr_ps[:, j * NV:(j + 1) * NV], xn_t[k][:, c, j * P:(j + 1) * P], wvr[:, c, :],
                                  start=(c == 0), stop=(c == C - 1))
                last.then_inc(vr_ready, 1)

            def queries_keys(k):
                for m in range(3):
                    rows_m = (P, P, KV * HD)[m]
                    if k:
                        pe.wait_ge(swapped, 3 * (k - 1) + m + 1)
                        pe.wait_ge(cos_done, 3 * (k - 1) + m + 1)
                    for c in range(C):
                        last = mm(pj_ps[m][0:rows_m, :], wqk[:, c, m * P:m * P + rows_m], xn_t[k][:, c, :],
                                  start=(c == 0), stop=(c == C - 1))
                    last.then_inc(pj_ready, 1)

            queries_keys(0)
            pe.wait_ge(choices_ready, 1)
            hot = onehot[:, :, :, :].rearrange("p k t e -> p (k t e)")
            mm(rank_ps[:, 0:2 * NT * E], earlier[:, :], hot, start=True, stop=True)
            mm(total_ps[:, 0:2 * NT * E], ones[:, :], hot, start=True, stop=True).then_inc(counts_ready, 1)
            for k in range(1, 2 * B):
                queries_keys(k)

            def score_max(h, p, a, i, taken):
                r, qt, kh = a // (2 * QT), a // 2 % QT, a % 2
                if taken is not None:
                    pe.wait_ge(mx_taken, taken)
                mm(mx_ps[i % 3], qa[h][:, r, qt * P:(qt + 1) * P], ka[p][:, kh * HALF:(kh + 1) * HALF],
                   start=True, stop=True).then_inc(mx_scored, 1)

            def turn_maxima(v, taken):
                pe.wait_ge(neg_mx_ready, v + 1)
                pe.wait_ge(mx_taken, taken)
                nc.tensor.transpose(mx_ps[TURN % 3][0:R * QT, 0:P], neg_mx[:, :], ident[:, :]).then_inc(mx_scored, 1)

            def first_max(n):
                v, a = n // NA, n % NA
                i = a + (a >= TURN)
                if a == 0:
                    pe.wait_ge(qa_loaded[v], 32)
                if v:
                    if a == TURN:
                        turn_maxima(0, uses_before(1) + TURN - 2)
                    score_max(1, 0, a, i, uses_before(1) + i - 2)
                else:
                    score_max(0, 0, a, i, a - 1 if a >= 2 else None)

            expert_reg = [pe.alloc_register(f"expert{i}") for i in range(4)]

            def load_expert(t, i):
                pe.reg_load(expert_reg[i], slot_ei[0:1, bass.ds(t, 1)])

            def expert_of(i):
                return pe.snap(expert_reg[i], min_val=0, max_val=E - 1)

            def to_columns(t, i):
                for c in range(C):
                    last = nc.tensor.transpose(xt_ps[i % 2][:, c * P:(c + 1) * P], rows[i][:, c * P:(c + 1) * P], ident[:, :])
                last.then_inc(xt_ready, 1)

            def gate_up(t, i):
                e = expert_of(i)
                pe.wait_ge(rows_t_ready, t + 1)
                for c in range(C):
                    last = mm(gu_ps[i % 2][:, :], rows_t[i % 2][:, c, :], wgu[:, e, c, :], start=(c == 0), stop=(c == C - 1))
                last.then_inc(gu_ready, 1)

            def act_columns(t, i, reused=True):
                pe.wait_ge(act_ready, t + 1)
                if reused:
                    pe.wait_ge(act_t_ready, t)
                for c in range(C):
                    last = nc.tensor.transpose(ht_ps[i % 2][:, c * P:(c + 1) * P], act_h[i % 2][:, c * P:(c + 1) * P], ident[:, :])
                last.then_inc(ht_ready, 1)

            def down(t, i, reused):
                e = expert_of(i)
                if reused:
                    pe.wait_ge(y_copied, t)
                pe.wait_ge(act_t_ready, t + 1)
                for c in range(C):
                    last = mm(y_ps[i % 2], act_t[i % 2][:, c, :], wdn[:, e, c, :], start=(c == 0), stop=(c == C - 1))
                last.then_inc(y_ready, 1)

            def expert(t, i, loads, first=False, last=False, beside=()):
                def products(n):
                    for x in n:
                        first_max(x)

                gate_up(t, i)
                products(beside[0:1])
                if not last:
                    load_expert(t + 1, (i + 1) % 4)
                if not first:
                    act_columns(t - 1, i - 1, not isinstance(t, int) or t >= 2)
                products(beside[1:2])
                if not last:
                    pe.wait_ge(rows_loaded[(i + 1) % 4], loads)
                    to_columns(t + 1, (i + 1) % 4)
                products(beside[2:3])
                if not isinstance(t, int) or t >= 2:
                    down(t - 2, (i - 2) % 4, not isinstance(t, int) or t >= 3)
                products(beside[3:])

            pe.wait_ge(places_ready, 1)
            load_expert(0, 0)
            pe.wait_ge(experts_loaded, 16 * 3 * C * E)
            pe.wait_ge(rows_loaded[0], 16)
            to_columns(0, 0)
            for t in range(8):
                expert(t, t % 4, 16 * ((t + 1) // 4 + 1), first=t == 0)
            with pe.Fori(2, (SLOTS - SHARED) // 4) as j:
                for i in range(4):
                    expert(4 * j + i, i, 16 * (j + 1 + (i + 1) // 4))
            pe.wait_ge(vec_made, 6)
            pe.wait_ge(stacks_padded, 4)
            pe.wait_ge(ka_loaded[0], 16)
            for t in range(SLOTS - SHARED, SLOTS):
                expert(t, t % 4, 16 * ((t + 1) // 4 + 1), last=t == SLOTS - 1, beside=shared_with(t))
            act_columns(SLOTS - 1, 3)
            for t in range(SLOTS - 2, SLOTS):
                down(t, t % 4, True)

            def scores(h, p, kt, s, j):
                if s is not None:
                    pe.wait_ge(exp_done, 2 * (s - 1) + j + 1)
                for r in (2 * j, 2 * j + 1):
                    last = mm(st_ps[j][:, (r - 2 * j) * HALF:(r - 2 * j + 1) * HALF],
                              kb[p][:, kt * P:(kt + 1) * P], qb[h][:, r, :], start=True, stop=True)
                last.then_inc(st_ready, 1)

            def values(p, kt, s, u):
                pe.wait_ge(exp_done, 2 * (s + 1))
                if kt == 0:
                    pe.wait_ge(o_free, u + 1)
                for r in range(R):
                    last = mm(o_ps[32 * r:32 * (r + 1), :], v_st[p][:, kt, :], probs[kt % 2][:, r, :],
                              start=(kt == 0), stop=(kt == KT - 1))
                last.then_inc(products_done, 1)

            pe.wait_ge(y_copied, SLOTS)
            pe.wait_ge(kb_loaded[0], 16)
            pe.wait_ge(qb_loaded[0], 64)
            for j in range(2):
                scores(0, 0, 0, None, j)

            def project_tile(t, chunks):
                for c in chunks:
                    if c == 0:
                        if t >= 3:
                            pe.wait_ge(fin_ready, t - 2)
                        if t == 0:
                            pe.wait_ge(wo_loaded, 16 * 2 * R)
                            pe.wait_ge(o_t_free, 2 + 2 * (G - 2) // 2)
                            pe.wait_ge(mx_taken, uses_before(2 * G) + 1)
                    if c == KC - 1 and t == KT:
                        pe.wait_ge(attn_ready, G - 1)
                    if c == KC - 1 and t == KT + QT:
                        pe.wait_ge(attn_ready, G)
                    last = mm(wo_ps[t % 3][:, 0:D], attn_t[:, c, t * P:(t + 1) * P], wo_s[:, c, :],
                              start=(c == 0), stop=(c == KC - 1))
                if chunks[-1] == KC - 1:
                    last.then_inc(wo_ready, 1)

            def project(n, kt):
                jobs = [(t, c) for t in out_tiles(n) for c in range(KC)]
                for t, c in jobs[len(jobs) * kt // KT:len(jobs) * (kt + 1) // KT]:
                    project_tile(t, [c])

            def group(g, p, last):
                for h in range(2):
                    u = 2 * g + h
                    n = uses_before(u + 2)

                    def maximum(a):
                        if not last:
                            if a == TURN:
                                turn_maxima(u + 1, n + TURN - 2)
                            i = a + (a >= TURN)
                            score_max(h, 1 - p, a, i, n + i - 2)

                    for kt in range(KT):
                        s = KT * u + kt
                        if not last and kt == 0:
                            pe.wait_ge(qa_loaded[h], 32 * (g + 2))
                            if h == 0:
                                pe.wait_ge(ka_loaded[1 - p], 16 * ((g - p) // 2 + p) + 16)
                        if last and h == 0 and kt == 0:
                            turn_maxima(u + 1, n)
                        if kt == KT - 1 and h == 0:
                            pe.wait_ge(qb_loaded[1], 64 * (g + 1))
                        if kt == KT - 1 and h == 1 and not last:
                            pe.wait_ge(kb_loaded[1 - p], 16 * ((g - p) // 2 + p) + 16)
                            pe.wait_ge(qb_loaded[0], 64 * (g + 2))
                        for j in range(2):
                            maximum(4 * kt + j)
                            if kt < KT - 1:
                                scores(h, p, kt + 1, s + 1, j)
                            elif h == 0:
                                scores(1, p, 0, s + 1, j)
                            elif not last:
                                scores(0, 1 - p, 0, s + 1, j)
                        maximum(4 * kt + 2)
                        maximum(4 * kt + 3)
                        if last:
                            project(h, kt)
                        if h == 0 and kt == 0:
                            pe.wait_ge(v_staged, g + 1)
                        values(p, kt, s, u)

            with pe.Fori(0, G // 2 - 1) as j:
                for p in range(2):
                    group(2 * j + p, p, False)
            group(G - 2, 0, False)
            group(G - 1, 1, True)

            for t in out_tiles(2):
                project_tile(t, range(KC))


def rope_tables(seq):
    half = HD // 2
    freqs = (np.float32(1.0) / np.power(np.float32(10000.0), np.arange(half, dtype=np.float32) / np.float32(half))).astype(np.float32)
    angles = np.arange(seq, dtype=np.float32)[:, None] * freqs[None, :]
    dims = np.arange(P) % HD
    sign = np.where(dims % 2 == 0, -1.0, 1.0).astype(np.float32)
    cos_t = np.cos(angles)[:, dims // 2].T
    sin_t = np.sin(angles)[:, dims // 2].T * sign[:, None]
    return np.ascontiguousarray(cos_t, np.float32), np.ascontiguousarray(sin_t, np.float32)


NAMES = ["L0_attn_x", "L0_attn_W_q", "L0_attn_W_k", "L0_attn_W_v", "L0_attn_W_o",
         "L0_ffn_Wr", "L0_ffn_Wg", "L0_ffn_Wu", "L0_ffn_Wd"]


def kernel(**inputs):
    import concourse.bacc as bacc
    from concourse.bass_utils import run_bass_kernel_spmd

    nc = bacc.Bacc("TRN2", target_bir_lowering=False, num_devices=1)
    arrays = {f"in_{n}": np.ascontiguousarray(inputs[n]) for n in NAMES}
    seq = arrays["in_L0_attn_x"].shape[1]
    arrays["rope_cos"], arrays["rope_sin"] = rope_tables(seq)
    args = [nc.dram_tensor(n, a.shape, F32, kind="ExternalInput").ap() for n, a in arrays.items()]
    out = nc.dram_tensor("out", arrays["in_L0_attn_x"].shape, F32, kind="ExternalOutput").ap()
    build(nc, *args, out)
    r = run_bass_kernel_spmd(nc, [arrays], core_ids=[0])
    return r.results[0]["out"]
```

```python
import math
from contextlib import ExitStack

import numpy as np

import concourse.bass as bass
from concourse import mybir

F32 = mybir.dt.float32
F32R = mybir.dt.float32r
BF16 = mybir.dt.bfloat16
I32 = mybir.dt.int32
U32 = mybir.dt.uint32
ALU = mybir.AluOpType
ACT = mybir.ActivationFunctionType
X_AXIS = mybir.AxisListType.X

P = 128
HD = 16
LN_EPS = 1e-5
CLAMP = 7.0
FAR = 3.0e38


def build(nc, x, w_q, w_k, w_v, w_o, w_r, w_g, w_u, w_d, cos_t, sin_t, out):
    B, S, D = x.shape
    C = D // P
    NH = w_q.shape[1] // HD
    KV = w_k.shape[1] // HD
    R = NH // KV
    E, _, F = w_g.shape
    NT = B * S // P
    ST_T = S // P
    G = B * KV
    HALF = S // 2
    KT = S // P
    QT = HALF // P
    TB = 4
    STACK = 4 * HD
    AUG = STACK + 2
    SLOTS = 2 * NT + E - 1
    NA = R * QT * 2
    TURN = 4
    NI = NA + 1
    NV = KV * HD + E
    assert C == 2 and R == 4 and KT == 8 and QT == 4 and E == 8 and HALF == 512 and F == 256
    assert B == 2 and TB * P == HALF

    xt = x.rearrange("b (t p) d -> p (b t) d", p=P)
    out_t = out.rearrange("b (t p) d -> p (b t) d", p=P)

    q_hl = nc.dram_tensor("q_hl", [B, NH, 2 * HD, S], F32, kind="Internal").ap()
    k_st = nc.dram_tensor("k_st", [B, KV, STACK, S], F32, kind="Internal").ap()
    xn_d = nc.dram_tensor("xn_d", [NT * P, D], F32, kind="Internal").ap()
    rows_out = nc.dram_tensor("rows_out", [SLOTS * P, D], F32, kind="Internal").ap()

    with ExitStack() as ctx:
        def sb(name, shape, dt=F32):
            return ctx.enter_context(nc.sbuf_tensor(name, shape, dt))

        def sem(name):
            return ctx.enter_context(nc.semaphore(name))

        big = sb("big", [P, E * C * 3 * F])
        wgu = big[:, 0:E * C * 2 * F].rearrange("p (e c n) -> p e c n", e=E, c=C)
        wdn = big[:, E * C * 2 * F:].rearrange("p (e c n) -> p e c n", e=E, c=C)
        KC = KV // 2
        attn_t = big[:, 0:KC * B * S].rearrange("p (c t) -> p c t", c=KC)
        probs = [big[:, KC * B * S + i * R * HALF:KC * B * S + (i + 1) * R * HALF]
                 .rearrange("p (r q) -> p r q", r=R) for i in range(2)]
        xs = sb("xs", [P, NT, D])
        xn = sb("xn", [P, NT, D])
        xn_t = [sb(f"xn_t{k}", [P, C, HALF]) for k in range(2 * B)]
        wqk = sb("wqk", [P, C, (NH + KV) * HD])
        wvr = sb("wvr", [P, C, KV * HD + E])
        wo_s = sb("wo_s", [P, KV // 2, D])
        cos_s = sb("cos_s", [P, S])
        sin_s = sb("sin_s", [P, S])
        rope_a = [sb(f"rope_a{m}", [P, HALF]) for m in range(3)]
        rope_b = [sb(f"rope_b{m}", [P, HALF]) for m in range(3)]
        rope_hi = [sb(f"rope_hi{m}", [P, HALF], F32R) for m in range(3)]
        rope_low = sb("rope_low", [P, 3, HALF], F32R)
        rope_lo = [rope_low[:, m, :] for m in range(3)]
        stats = [sb(f"stats{h}", [P, TB, 6]) for h in range(2)]
        mean_var = [sb(f"mean_var{h}", [P, TB, 2]) for h in range(2)]
        std = [sb(f"std{h}", [P, TB]) for h in range(2)]
        rstd = [sb(f"rstd{h}", [P, TB]) for h in range(2)]
        neg_shift = [sb(f"neg_shift{h}", [P, TB]) for h in range(2)]
        eps = sb("eps", [P, 1])
        v_all = sb("v_all", [P, NT, KV * HD])
        ident = sb("ident", [P, P])
        earlier = sb("earlier", [P, P])
        ones = sb("ones", [P, P])
        logits = sb("logits", [P, NT, E])
        logits2 = sb("logits2", [P, NT, E])
        expert_no = sb("expert_no", [P, 2 * NT, E])
        cand = sb("cand", [P, NT, E])
        top = sb("top", [P, 2, NT])
        choice = sb("choice", [P, 2, NT])
        onehot = sb("onehot", [P, 2, NT, E])
        gate = sb("gate", [P, 2, NT])
        gate_t = sb("gate_t", [P, 3, NT])
        sums = [sb(f"sums{i}", [P, 2 * NT, E]) for i in range(2)]
        totals = sb("totals", [P, 2 * NT, E])
        limit = sb("limit", [P, E, NT])
        over = sb("over", [P, E, NT])
        n_tiles = sb("n_tiles", [P, E])
        cum = [sb(f"cum{i}", [P, E]) for i in range(2)]
        slot_no = sb("slot_no", [P, SLOTS, E])
        slot_ge = sb("slot_ge", [P, SLOTS, E])
        slot_e = sb("slot_e", [P, SLOTS])
        slot_ei = sb("slot_ei", [P, SLOTS], I32)
        place = sb("place", [P, 2 * NT])
        place_i = sb("place_i", [P, 2 * NT], U32)
        place_parts = [sb(f"place_part{i}", [P, 2 * NT], U32) for i in range(2)]
        place_tile = sb("place_tile", [P, 2 * NT])
        place_row = sb("place_row", [P, 2 * NT])
        tile_first = sb("tile_first", [P, 2 * NT])
        partition_no = sb("partition_no", [P, 1])
        row_no = sb("row_no", [P, P])
        token_of = sb("token_of", [P, SLOTS], U32)
        token_part = sb("token_part", [P, SLOTS])
        spare = xn[:, :, :].rearrange("p t d -> p (t d)")

        def in_spare(n, width):
            return spare[:, n * width:(n + 1) * width]

        rows = [in_spare(i, D) for i in range(4)]
        rows_t = [in_spare(4 + i, D).rearrange("p (c n) -> p c n", c=C) for i in range(2)]
        act_g = [in_spare(6 + i, F) for i in range(2)]
        act_h = [in_spare(8 + i, F) for i in range(2)]
        act_t = [in_spare(10 + i, F).rearrange("p (c n) -> p c n", c=C) for i in range(2)]
        y_s = [in_spare(12 + i, D) for i in range(4)]
        o_q = in_spare(2, HALF)
        o_n = [in_spare(3 + h, HALF) for h in range(2)]
        o_t = [in_spare(h, HALF) for h in range(2)]
        qa = [sb(f"qa{h}", [P, R, HALF], F32R) for h in range(2)]
        qb = [sb(f"qb{h}", [P, R, HALF], F32R) for h in range(2)]
        ka = [sb(f"ka{p}", [P, S], F32R) for p in range(2)]
        kb = [sb(f"kb{p}", [P, S], F32R) for p in range(2)]
        v_st = [sb(f"v_st{p}", [P, KT, 32]) for p in range(2)]
        mx = [sb(f"mx{h}", [P, R * QT, 2]) for h in range(2)]
        neg_mx = sb("neg_mx", [P, R * QT])
        m_hi = [sb(f"m_hi{h}", [R * QT, P], F32R) for h in range(2)]
        m_lo = [sb(f"m_lo{h}", [R * QT, P], F32R) for h in range(2)]
        rden = sb("rden", [P, HALF // 32])

        in_row = spare.bitcast(BF16)[:, 0:2 * NT * P].rearrange("p (n w) -> p n w", w=P)
        in_tile = rope_low[:, :, :].rearrange("p m q -> p (m q)").bitcast(BF16)[:, 0:2 * NT * 2 * SLOTS].rearrange(
            "p (n s w) -> p n s w", s=2, w=SLOTS)
        hot_tile = spare.bitcast(BF16)[:, 2 * NT * P:2 * NT * (P + SLOTS)].rearrange("p (n w) -> p n w", w=SLOTS)
        y_got = [rope_a[0][:, k * D:(k + 1) * D] for k in range(2)]
        fin = [rope_a[1 + i // 2][:, i % 2 * D:(i % 2 + 1) * D] for i in range(4)]

        bank = [ctx.enter_context(nc.psum_tensor(f"bank{i}", [P, 1024], F32)) for i in range(4)]

        def half_bank(i):
            return bank[i // 2][:, 512 * (i % 2):512 * (i % 2) + 512]

        tr_ps = [half_bank(0), half_bank(1)]
        vr_ps = [half_bank(2 + k) for k in range(4)]
        pj_ps = [[half_bank(i) for i in ((4, 5, 6) if k % 2 else (0, 1, 3))] for k in range(2 * B)]
        inverse_ps = half_bank(2)[:, 0:2 * SLOTS]
        rank_ps = half_bank(7)[:, 0:2 * NT * E]
        total_ps = half_bank(7)[:, 2 * NT * E:4 * NT * E]
        xt_ps = [half_bank(0)[:, i * D:(i + 1) * D] for i in range(2)]
        ht_ps = [half_bank(1)[:, i * F:(i + 1) * F] for i in range(2)]
        gu_ps = [half_bank(2), half_bank(3)]
        y_ps = [half_bank(7)[:, i * D:(i + 1) * D] for i in range(2)]
        last_y_ps = gu_ps[SLOTS % 2][:, 0:D]
        st_ps = [bank[0], bank[1]]
        mx_ps = [half_bank(4), half_bank(5), half_bank(6)]
        o_ps = half_bank(7)
        wo_ps = mx_ps

        def side(o, s):
            return o.rearrange("p (n d) -> p n d", d=32)[:, :, HD * s:HD * (s + 1)]

        x_loaded = [sem(f"x_loaded{k}") for k in range(4)]
        small_loaded = sem("small_loaded")
        wo_loaded = sem("wo_loaded")
        experts_loaded = sem("experts_loaded")
        xn_stored = sem("xn_stored")
        pool_made = sem("pool_made")
        stacks_padded = sem("stacks_padded")
        dve_ln = sem("dve_ln")
        stats_ready = sem("stats_ready")
        std_ready = sem("std_ready")
        shift_ready = sem("shift_ready")
        xn_ready = sem("xn_ready")
        tr_ready = sem("tr_ready")
        xn_t_ready = sem("xn_t_ready")
        vr_ready = sem("vr_ready")
        vr_taken = sem("vr_taken")
        pj_ready = sem("pj_ready")
        pj_copied = sem("pj_copied")
        swapped = sem("swapped")
        cos_done = sem("cos_done")
        sin_done = sem("sin_done")
        rope_done = sem("rope_done")
        hi_ready = sem("hi_ready")
        lo_ready = sem("lo_ready")
        qk_stored = [sem(f"qk_stored{m}") for m in range(3)]
        route = sem("route")
        choices_ready = sem("choices_ready")
        counts_ready = sem("counts_ready")
        diff_ready = sem("diff_ready")
        gate_exp = sem("gate_exp")
        gates_ready = sem("gates_ready")
        experts_known = sem("experts_known")
        hot_tile_ready = sem("hot_tile_ready")
        in_tile_ready = sem("in_tile_ready")
        in_row_ready = sem("in_row_ready")
        inverse_ready = sem("inverse_ready")
        tokens_ready = sem("tokens_ready")
        rows_loaded = [sem(f"rows_loaded{i}") for i in range(4)]
        xt_ready = sem("xt_ready")
        rows_t_ready = sem("rows_t_ready")
        gu_ready = sem("gu_ready")
        silu_ready = sem("silu_ready")
        clip_done = sem("clip_done")
        act_ready = sem("act_ready")
        ht_ready = sem("ht_ready")
        act_t_ready = sem("act_t_ready")
        y_ready = sem("y_ready")
        y_copied = sem("y_copied")
        y_stored = [sem(f"y_stored{i}") for i in range(4)]
        qa_loaded = [sem(f"qa_loaded{h}") for h in range(2)]
        qb_loaded = [sem(f"qb_loaded{h}") for h in range(2)]
        ka_loaded = [sem(f"ka_loaded{p}") for p in range(2)]
        kb_loaded = [sem(f"kb_loaded{p}") for p in range(2)]
        v_staged = sem("v_staged")
        mx_scored = sem("mx_scored")
        mx_taken = sem("mx_taken")
        neg_mx_ready = sem("neg_mx_ready")
        m_hi_ready = sem("m_hi_ready")
        st_ready = sem("st_ready")
        exp_done = sem("exp_done")
        products_done = sem("products_done")
        o_free = sem("o_free")
        rden_ready = sem("rden_ready")
        divided = sem("divided")
        attn_ready = sem("attn_ready")
        o_t_free = sem("o_t_free")
        y_gathered = sem("y_gathered")
        mix = sem("mix")
        wo_ready = sem("wo_ready")
        fin_ready = sem("fin_ready")
        stored = [sem(f"stored{i}") for i in range(4)]

        BLOCKS = 2 * B
        PARTS = [(k, 2) for k in range(BLOCKS - 1)] + [(k, m) for k in range(BLOCKS) for m in range(2)] + [(BLOCKS - 1, 2)]
        NP = len(PARTS)
        VECTOR_COS = (3, 5, 7)
        AHEAD = 2

        def part_rows(q):
            return P if PARTS[q][1] < 2 else KV * HD

        def vector_cos(q):
            return PARTS[q][0] == BLOCKS - 1 or q in VECTOR_COS

        def projected(k, m):
            if k == BLOCKS - 1:
                return pj_ps[k][m]
            return xn_t[k][:, m, :] if m < 2 else rope_hi[k][:, :].bitcast(F32)

        def stored_before(q):
            return sum(32 if PARTS[o][1] < 2 else 64 for o in range(q % 3, q, 3))

        SHARED = 15

        def shared_with(t):
            n = t - (SLOTS - SHARED)
            return list(range(2 * NA * n // SHARED, 2 * NA * (n + 1) // SHARED))

        def out_tiles(n):
            return (range(0, KT), range(KT, KT + QT), range(KT + QT, NT))[n]

        def uses_before(v):
            return NI * v - 1

        block = ctx.enter_context(nc.Block())

        @block.sync
        def _(sp):
            for k in range(2 * B):
                sp.dma_start(xs[:, k * TB:(k + 1) * TB, :], xt[:, k * TB:(k + 1) * TB, :]).then_inc(x_loaded[k], 16)
            wo_rows = w_o.rearrange("(r c s d) n -> r s d c n", r=R, s=2, d=HD)
            with sp.Fori(0, E) as e:
                for c in range(C):
                    sp.dma_start(wgu[:, e, c, 0:F], w_g[e, c * P:(c + 1) * P, :]).then_inc(experts_loaded, 16)
                    sp.dma_start(wgu[:, e, c, F:2 * F], w_u[e, c * P:(c + 1) * P, :]).then_inc(experts_loaded, 16)
                    sp.dma_start(wdn[:, e, c, :], w_d[e, c * P:(c + 1) * P, :]).then_inc(experts_loaded, 16)

            for r in range(R):
                for s in range(2):
                    sp.dma_start(wo_s[32 * r + HD * s:32 * r + HD * (s + 1), :, :], wo_rows[r, s]).then_inc(wo_loaded, 16)

            def store_part(q):
                k, m = PARTS[q]
                n, done = q % 3, qk_stored[q % 3]
                b, cols = k // 2, slice(k % 2 * HALF, (k % 2 + 1) * HALF)
                sp.wait_ge(lo_ready, q + 1)
                if m < 2:
                    q_rows = q_hl[b, 8 * m:8 * m + 8, :, cols].rearrange("n (s d) q -> s n d q", s=2)
                    sp.dma_start(q_rows[0], rope_hi[n][:, :].bitcast(F32)).then_inc(done, 16)
                    sp.dma_start(q_rows[1], rope_lo[n].bitcast(F32)).then_inc(done, 16)
                else:
                    for j, half in enumerate((rope_hi, rope_hi, rope_lo, rope_lo)):
                        sp.dma_start(k_st[b, :, HD * j:HD * (j + 1), cols],
                                     half[n][0:KV * HD, :].bitcast(F32)).then_inc(done, 16)

            def store_y(t, i):
                sp.wait_ge(y_copied, t + 1)
                sp.dma_start(rows_out[bass.ts(t, P), :], y_s[i]).then_inc(y_stored[i], 16)

            for q in range(NP):
                store_part(q)
                if q >= 2:
                    store_y(q - 2, (q - 2) % 4)
            for t in range(NP - 2, NP):
                store_y(t, t % 4)

            def load_q(dst, done, g, h):
                b, kv = g // KV, g % KV
                src = q_hl[b].rearrange("(r k) d q -> k d r q", k=KV)[kv][:, :, h * HALF:(h + 1) * HALF]
                for j in range(2):
                    sp.dma_start(dst[h][2 * HD * j:2 * HD * (j + 1), :, :].bitcast(F32), src).then_inc(done[h], 16)

            def load_k(dst, done, g, p):
                sp.dma_start(dst[p][0:STACK, :].bitcast(F32), k_st[g // KV, g % KV]).then_inc(done[p], 16)

            def load_m(h):
                for row, part in ((STACK, m_hi), (STACK + 1, m_lo)):
                    sp.dma_start(qb[h][row:row + 1, :, :].rearrange("o r (t c) -> o (r t) c", c=P).bitcast(F32),
                                 part[h][:, :].bitcast(F32)).then_inc(qb_loaded[h], 16)


            for m in range(3):
                sp.wait_ge(qk_stored[m], stored_before(NP + m))
            load_k(ka, ka_loaded, 0, 0)
            for h in range(2):
                load_q(qa, qa_loaded, 0, h)
            load_k(ka, ka_loaded, 1, 1)
            load_k(kb, kb_loaded, 0, 0)
            for h in range(2):
                load_q(qb, qb_loaded, 0, h)
            with sp.Fori(NP // 4, SLOTS // 4 - 2) as j:
                for i in range(4):
                    store_y(4 * j + i, i)
            for t in range(4 * (SLOTS // 4 - 2), SLOTS - 9):
                store_y(t, t % 4)
            sp.wait_ge(mx_scored, uses_before(1))
            load_q(qa, qa_loaded, 1, 0)
            for t in range(SLOTS - 9, SLOTS - 7):
                store_y(t, t % 4)
            sp.wait_ge(mx_taken, uses_before(1) + TURN + 1)
            load_m(0)
            for t in range(SLOTS - 7, SLOTS - 2):
                store_y(t, t % 4)
            sp.wait_ge(mx_scored, uses_before(2))
            load_q(qa, qa_loaded, 1, 1)
            for t in range(SLOTS - 2, SLOTS):
                store_y(t, t % 4)

            def period(g, p, last):
                if not last:
                    load_k(ka, ka_loaded, g + 2, p)
                sp.wait_ge(st_ready, 2 * KT * 2 * g + 1)
                load_k(kb, kb_loaded, g + 1, 1 - p)
                for h in range(2):
                    u = 2 * g + h
                    sp.wait_ge(mx_taken, uses_before(u + 2) + TURN + 1)
                    load_m(1 - h)
                    sp.wait_ge(st_ready, 2 * KT * (u + 1))
                    load_q(qb, qb_loaded, g + 1, h)
                    if not last:
                        sp.wait_ge(mx_scored, uses_before(u + 3))
                        load_q(qa, qa_loaded, g + 2, h)

            with sp.Fori(0, G // 2 - 1) as j:
                for p in range(2):
                    period(2 * j + p, p, False)
            period(G - 2, 0, True)
            sp.wait_ge(mx_taken, uses_before(2 * G) + 1)
            load_m(1)

            for t in range(NT):
                sp.wait_ge(fin_ready, t + 1)
                sp.dma_start(out_t[:, t, :], fin[t % 4]).then_inc(stored[t % 4], 16)
            for i in range(4):
                sp.wait_ge(stored[i], 16 * NT // 4)

        @block.gpsimd
        def _(pool):
            pool.memset(ident[:, :], 0.0).then_inc(pool_made, 1)
            pool.memset(earlier[:, :], 1.0).then_inc(pool_made, 1)
            pool.memset(ones[:, :], 1.0).then_inc(pool_made, 1)
            pool.wait_ge(pool_made, 3)
            pool.affine_select(out=ident[:, :], in_=ident[:, :], compare_op=ALU.not_equal, fill=1.0,
                               base=0, pattern=[[-1, P]], channel_multiplier=1).then_inc(pool_made, 1)
            pool.affine_select(out=earlier[:, :], in_=earlier[:, :], compare_op=ALU.is_gt, fill=0.0,
                               base=0, pattern=[[1, P]], channel_multiplier=-1).then_inc(pool_made, 1)
            pool.memset(eps[:, :], LN_EPS).then_inc(pool_made, 1)
            pool.iota(expert_no[:, :, :], pattern=[[0, 2 * NT], [1, E]], base=0, channel_multiplier=0,
                      allow_small_or_imprecise_dtypes=True).then_inc(pool_made, 1)
            pool.iota(limit[:, :, :], pattern=[[0, E], [P, NT]], base=0, channel_multiplier=0,
                      allow_small_or_imprecise_dtypes=True).then_inc(pool_made, 1)
            pool.iota(slot_no[:, :, :], pattern=[[1, SLOTS], [0, E]], base=0, channel_multiplier=0,
                      allow_small_or_imprecise_dtypes=True).then_inc(pool_made, 1)
            pool.iota(tile_first[:, :], pattern=[[0, 2], [P, NT]], base=0, channel_multiplier=0,
                      allow_small_or_imprecise_dtypes=True).then_inc(pool_made, 1)
            pool.iota(row_no[:, :], pattern=[[1, P]], base=0, channel_multiplier=0,
                      allow_small_or_imprecise_dtypes=True).then_inc(pool_made, 1)
            pool.iota(partition_no[:, :], pattern=[[0, 1]], base=0, channel_multiplier=1,
                      allow_small_or_imprecise_dtypes=True).then_inc(pool_made, 1)
            for p in range(2):
                pool.memset(v_st[p][:, :, HD + 1:], 0.0).then_inc(pool_made, 1)
                pool.memset(v_st[p][:, :, HD:HD + 1], 1.0).then_inc(pool_made, 1)
            pool.wait_ge(pool_made, 16)
            for n, q in enumerate(qa + qb):
                pool.memset(q[STACK:P, :, :].bitcast(F32), 0.0).then_inc(stacks_padded, 1)
                pool.wait_ge(stacks_padded, n + 1)
            for n, k in enumerate(ka + kb):
                pool.memset(k[STACK:P, :].bitcast(F32), 0.0).then_inc(stacks_padded, 1)
                pool.wait_ge(stacks_padded, 4 + n + 1)
            for n, k in enumerate(kb):
                pool.memset(k[STACK:AUG, :].bitcast(F32), 1.0).then_inc(stacks_padded, 1)
                pool.wait_ge(stacks_padded, 8 + n + 1)
            pool.sem_inc(o_t_free, 2)

            def gather_rows(t):
                pool.indirect_dma_start(
                    out=rows[t % 4], out_offset=None, in_=xn_d[:, :],
                    in_offset=bass.IndirectOffsetOnAxis(ap=token_of[:, t:t + 1], axis=0)).then_inc(rows_loaded[t % 4], 16)

            def times_cos(q):
                (k, m), n, rows_q = PARTS[q], q % 3, part_rows(q)
                if not vector_cos(q):
                    pool.wait_ge(pj_copied, 3 * k + m + 1)
                    if q >= 3:
                        pool.wait_ge(hi_ready, q - 2)
                        pool.wait_ge(lo_ready, q - 2)
                    pool.tensor_tensor(rope_a[n][0:rows_q, :], projected(k, m)[0:rows_q, :],
                                       cos_s[0:rows_q, k % 2 * HALF:(k % 2 + 1) * HALF], ALU.mult).then_inc(cos_done, 1)

            def times_sin(q):
                (k, m), n, rows_q = PARTS[q], q % 3, part_rows(q)
                pool.wait_ge(swapped, q + 1)
                pool.tensor_tensor(rope_b[n][0:rows_q, :], rope_b[n][0:rows_q, :],
                                   sin_s[0:rows_q, k % 2 * HALF:(k % 2 + 1) * HALF], ALU.mult).then_inc(sin_done, 1)

            pool.wait_ge(small_loaded, 16 * 6)
            for q in range(2):
                times_cos(q)
            pool.wait_ge(hot_tile_ready, 1)
            pool.tensor_tensor(in_tile[:, :, 0, :], hot_tile, tile_first[:, :].unsqueeze(2).to_broadcast([P, 2 * NT, SLOTS]),
                               ALU.mult).then_inc(in_tile_ready, 1)
            times_cos(2)
            pool.wait_ge(xn_stored, 16 * 2 * B)
            pool.wait_ge(tokens_ready, 1)
            for t in range(4):
                gather_rows(t)
                if t < AHEAD:
                    times_sin(t)
            for t in range(4, SLOTS):
                pool.wait_ge(xt_ready, t - 3)
                gather_rows(t)
                q = t - 4 + AHEAD
                if q < NP:
                    if q >= 3:
                        times_cos(q)
                    times_sin(q)

            def stage_v(g, p):
                pool.tensor_copy(v_st[p][:, :, 0:HD],
                                 v_all[:, (g // KV) * ST_T:(g // KV + 1) * ST_T, (g % KV) * HD:(g % KV + 1) * HD]).then_inc(v_staged, 1)

            pool.wait_ge(vr_taken, 4 * B)
            stage_v(0, 0)
            stage_v(1, 1)

            pool.wait_ge(gates_ready, 1)
            for i in range(4):
                pool.wait_ge(y_stored[i], 16 * len(range(i, SLOTS, 4)))

            def mix_tile(t):
                for k in range(2):
                    pool.indirect_dma_start(
                        out=y_got[k][:, :], out_offset=None, in_=rows_out[:, :],
                        in_offset=bass.IndirectOffsetOnAxis(ap=place_i[:, k * NT + t:k * NT + t + 1], axis=0)
                    ).then_inc(y_gathered, 16)
                pool.wait_ge(y_gathered, 32 * (t + 1))
                for k in range(2):
                    pool.tensor_scalar(y_got[k][:, :], y_got[k][:, :], gate[:, k, t:t + 1], None,
                                       ALU.mult).then_inc(mix, 1)
                pool.wait_ge(mix, 4 * t + 2)
                pool.tensor_tensor(y_got[0][:, :], y_got[0][:, :], y_got[1][:, :], ALU.add).then_inc(mix, 1)
                pool.wait_ge(mix, 4 * t + 3)
                pool.tensor_tensor(xs[:, t, :], xs[:, t, :], y_got[0][:, :], ALU.add).then_inc(mix, 1)
                pool.wait_ge(mix, 4 * t + 4)

            MIX_UNITS = 12
            for u in range(2 * G - 1):
                g, h = u // 2, u % 2
                pool.wait_ge(rden_ready, u + 1)
                if g % 2 == 0 and g:
                    pool.wait_ge(attn_ready, g - 1 + h)
                pool.tensor_tensor(side(o_n[h], g % 2), side(o_q, 0),
                                   rden[:, :].unsqueeze(2).to_broadcast([P, HALF // 32, HD]), ALU.mult).then_inc(divided, 1)
                if u < MIX_UNITS:
                    for t in range(u * NT // MIX_UNITS, (u + 1) * NT // MIX_UNITS):
                        mix_tile(t)
                if g % 2 and g < G - 1:
                    pool.wait_ge(attn_ready, g + h)
                    q0 = g // KV * S + h * HALF
                    pool.tensor_copy(attn_t[:, g % KV // 2, q0:q0 + HALF], o_t[h]).then_inc(o_t_free, 1)
                if h and g < G - 2:
                    pool.wait_ge(products_done, 2 * KT * (g + 1))
                    stage_v(g + 2, g % 2)

        @block.scalar
        def _(act):
            def by_chunk(w):
                return w.rearrange("(c p) n -> p c n", p=P)

            act.dma_start(wvr[:, :, 0:KV * HD], by_chunk(w_v)).then_inc(small_loaded, 16)
            act.dma_start(wvr[:, :, KV * HD:], by_chunk(w_r)).then_inc(small_loaded, 16)
            act.dma_start(wqk[:, :, 0:NH * HD], by_chunk(w_q)).then_inc(small_loaded, 16)
            act.dma_start(wqk[:, :, NH * HD:], by_chunk(w_k)).then_inc(small_loaded, 16)
            act.dma_start(cos_s[:, :], cos_t).then_inc(small_loaded, 16)
            act.dma_start(sin_s[:, :], sin_t).then_inc(small_loaded, 16)

            def copy_columns(k):
                for c in range(C):
                    act.wait_ge(tr_ready, C * k + c + 1)
                    act.activation(xn_t[k][:, c, :], tr_ps[c], ACT.Copy).then_inc(xn_t_ready, 1)
                act.wait_ge(xn_ready, 2 * (k + 1))
                act.dma_start(xn_d[k * TB * P:(k + 1) * TB * P, :].rearrange("(t p) d -> p t d", p=P),
                              xn[:, k * TB:(k + 1) * TB, :]).then_inc(xn_stored, 16)

            act.wait_ge(pool_made, 6)
            for k in range(2 * B):
                act.wait_ge(stats_ready, k + 1)
                act.activation(std[k % 2][:, :], mean_var[k % 2][:, :, 1], ACT.Sqrt, bias=eps[:, 0:1]).then_inc(std_ready, 1)
                act.wait_ge(shift_ready, k + 1)
                for j in range(TB // 2, TB):
                    last = act.activation(xn[:, k * TB + j, :], xs[:, k * TB + j, :], ACT.Identity,
                                          bias=neg_shift[k % 2][:, j:j + 1], scale=rstd[k % 2][:, j:j + 1])
                last.then_inc(xn_ready, 1)
                if k:
                    copy_columns(k - 1)
            copy_columns(2 * B - 1)
            act.wait_ge(diff_ready, 1)
            act.activation(gate_t[:, 1, :], gate_t[:, 0, :], ACT.Exp).then_inc(gate_exp, 1)
            for k in range(BLOCKS - 1):
                act.wait_ge(pj_ready, 3 * (k + 1))
                for m in range(3):
                    rows_m = (P, P, KV * HD)[m]
                    act.activation(projected(k, m)[0:rows_m, :], pj_ps[k][m][0:rows_m, :], ACT.Copy).then_inc(pj_copied, 1)

            act.wait_ge(hot_tile_ready, 1)
            act.activation(in_tile[:, :, 1, :], hot_tile, ACT.Copy, scale=partition_no[:, 0:1]).then_inc(in_tile_ready, 1)

            def high_part(q):
                n, rows_q = q % 3, part_rows(q)
                act.wait_ge(rope_done, q + 1)
                if q >= 3:
                    act.wait_ge(qk_stored[n], stored_before(q))
                act.activation(rope_hi[n][0:rows_q, :], rope_a[n][0:rows_q, :], ACT.Copy).then_inc(hi_ready, 1)

            def expert(t, i, first=False, last=False):
                act.wait_ge(gu_ready, t + 1)
                act.activation(act_g[i], gu_ps[i][:, 0:F], ACT.Silu).then_inc(silu_ready, 1)
                if not last:
                    act.wait_ge(xt_ready, t + 2)
                    act.activation(rows_t[1 - i].rearrange("p c n -> p (c n)"), xt_ps[1 - i],
                                   ACT.Copy).then_inc(rows_t_ready, 1)
                if not first:
                    act.wait_ge(ht_ready, t)
                    act.activation(act_t[1 - i].rearrange("p c n -> p (c n)"), ht_ps[1 - i],
                                   ACT.Copy).then_inc(act_t_ready, 1)

            act.wait_ge(xt_ready, 1)
            act.activation(rows_t[0].rearrange("p c n -> p (c n)"), xt_ps[0],
                           ACT.Copy).then_inc(rows_t_ready, 1)
            for q in range(AHEAD - 1):
                high_part(q)
            for t in range(NP):
                expert(t, t % 2, first=t == 0)
                if t + AHEAD - 1 < NP:
                    high_part(t + AHEAD - 1)
            with act.Fori(NP // 2, SLOTS // 2 - 1) as j:
                for i in range(2):
                    expert(2 * j + i, i)
            for t in range(2 * (SLOTS // 2 - 1), SLOTS):
                expert(t, t % 2, last=t == SLOTS - 1)
            act.wait_ge(ht_ready, SLOTS)
            act.activation(act_t[(SLOTS - 1) % 2].rearrange("p c n -> p (c n)"), ht_ps[(SLOTS - 1) % 2],
                           ACT.Copy).then_inc(act_t_ready, 1)

            def exps(u, first=False):
                for kt in range(KT):
                    s = KT * u + kt
                    if not first or kt >= 2:
                        act.wait_ge(products_done, s - 1)
                    for j in range(2):
                        act.wait_ge(st_ready, 2 * s + j + 1)
                        act.activation(probs[kt % 2][:, 2 * j:2 * j + 2, :].rearrange("p r q -> p (r q)"),
                                       st_ps[j][:, :], ACT.Exp, scale=1.0 / math.sqrt(HD)).then_inc(exp_done, 1)

            exps(0, True)
            with act.Fori(1, 2 * G) as u:
                exps(u)

        @block.vector
        def _(dve):
            dve.sem_inc(o_free, 1)
            for b in range(B):
                for h in range(2):
                    k = 2 * b + h
                    t0 = b * ST_T + h * TB
                    N_LN = 2
                    dve.wait_ge(x_loaded[k], 16)
                    if k >= 2:
                        dve.wait_ge(xn_ready, 2 * (k - 1))
                    for j in range(TB):
                        last = nc.vector.bn_stats(stats[h][:, j, :], xs[:, t0 + j, :])
                    last.then_inc(dve_ln, 1)
                    dve.wait_ge(dve_ln, N_LN * k + 1)
                    for j in range(TB):
                        last = nc.vector.bn_aggr(mean_var[h][:, j, :], stats[h][:, j, :])
                    last.then_inc(stats_ready, 1)
                    dve.wait_ge(std_ready, k + 1)
                    nc.vector.reciprocal(rstd[h][:, :], std[h][:, :]).then_inc(dve_ln, 1)
                    dve.wait_ge(dve_ln, N_LN * k + 2)
                    dve.wait_ge(stats_ready, k + 1)
                    nc.vector.scalar_tensor_tensor(neg_shift[h][:, :], mean_var[h][:, :, 0], -1.0, rstd[h][:, :],
                                                   ALU.mult, ALU.mult).then_inc(shift_ready, 1)
                    for j in range(TB // 2):
                        last = nc.vector.tensor_scalar(xn[:, t0 + j, :], xs[:, t0 + j, :], mean_var[h][:, j, 0:1],
                                                       rstd[h][:, j:j + 1], ALU.subtract, ALU.mult)
                    last.then_inc(xn_ready, 1)
            for b in range(B):
                for h in range(2):
                    k = 2 * b + h
                    t0 = b * ST_T + h * TB
                    dve.wait_ge(vr_ready, k + 1)
                    vr = vr_ps[k][:, 0:TB * (KV * HD + E)].rearrange("p (t n) -> p t n", t=TB)
                    nc.vector.tensor_copy(v_all[:, t0:t0 + TB, :], vr[:, :, 0:KV * HD]).then_inc(vr_taken, 1)
                    nc.vector.tensor_copy(logits[:, t0:t0 + TB, :], vr[:, :, KV * HD:]).then_inc(vr_taken, 1)

            n_route = [0]

            def link(ins):
                ins.then_inc(route, 1)
                n_route[0] += 1
                dve.wait_ge(route, n_route[0])

            dve.wait_ge(pool_made, 12)
            dve.wait_ge(vr_taken, 4 * B)
            numbers = expert_no[:, 0:NT, :]

            def pick(lg, k):
                link(nc.vector.tensor_reduce(top[:, k, :], lg[:, :, :], X_AXIS, ALU.max))
                link(nc.vector.tensor_tensor(cand[:, :, :], lg[:, :, :],
                                             top[:, k, :].unsqueeze(2).to_broadcast([P, NT, E]), ALU.is_ge))
                link(nc.vector.scalar_tensor_tensor(cand[:, :, :], cand[:, :, :], -float(E), numbers,
                                                    ALU.mult, ALU.add))
                link(nc.vector.tensor_reduce(choice[:, k, :], cand[:, :, :], X_AXIS, ALU.min))
                link(nc.vector.tensor_tensor(onehot[:, k, :, :], cand[:, :, :],
                                             choice[:, k, :].unsqueeze(2).to_broadcast([P, NT, E]), ALU.is_equal))

            pick(logits, 0)
            link(nc.vector.scalar_tensor_tensor(logits2[:, :, :], onehot[:, 0, :, :], -FAR, logits[:, :, :],
                                                ALU.mult, ALU.add))
            pick(logits2, 1)
            nc.vector.engine_nop().then_inc(choices_ready, 1)
            nc.vector.tensor_tensor(gate_t[:, 0, :], top[:, 1, :], top[:, 0, :], ALU.subtract).then_inc(diff_ready, 1)

            flat = "p t e -> p (t e)"
            dve.wait_ge(counts_ready, 1)
            link(nc.vector.tensor_copy(sums[0][:, :, :].rearrange(flat), total_ps))
            src, step = 0, 1
            while step < 2 * NT:
                a, z = sums[src], sums[1 - src]
                nc.vector.tensor_copy(z[:, 0:step, :], a[:, 0:step, :])
                link(nc.vector.tensor_tensor(z[:, step:, :], a[:, step:, :], a[:, 0:2 * NT - step, :], ALU.add))
                src, step = 1 - src, 2 * step
            incl = sums[src]
            link(nc.vector.tensor_tensor(over[:, :, :], incl[:, 2 * NT - 1, :].unsqueeze(2).to_broadcast([P, E, NT]),
                                         limit[:, :, :], ALU.is_gt))
            link(nc.vector.reduce_sum(n_tiles[:, :], over[:, :, :], axis=X_AXIS))
            csrc, step = 1, 1
            while step < E:
                a, z = cum[csrc] if step > 1 else n_tiles, cum[1 - csrc]
                nc.vector.tensor_copy(z[:, 0:step], a[:, 0:step])
                link(nc.vector.tensor_tensor(z[:, step:], a[:, step:], a[:, 0:E - step], ALU.add))
                csrc, step = 1 - csrc, 2 * step
            ends = cum[csrc]
            link(nc.vector.tensor_tensor(n_tiles[:, :], ends[:, :], n_tiles[:, :], ALU.subtract))
            link(nc.vector.tensor_scalar(n_tiles[:, :], n_tiles[:, :], float(P), None, ALU.mult))
            link(nc.vector.tensor_tensor(totals[:, :, :].rearrange(flat), incl[:, :, :].rearrange(flat), total_ps, ALU.subtract))
            link(nc.vector.tensor_tensor(totals[:, :, :].rearrange(flat), totals[:, :, :].rearrange(flat),
                                         rank_ps, ALU.add))
            link(nc.vector.tensor_tensor(totals[:, :, :], totals[:, :, :],
                                         n_tiles[:, :].unsqueeze(1).to_broadcast([P, 2 * NT, E]), ALU.add))
            link(nc.vector.tensor_tensor(totals[:, :, :].rearrange(flat), totals[:, :, :].rearrange(flat),
                                         onehot[:, :, :, :].rearrange("p k t e -> p (k t e)"), ALU.mult))
            link(nc.vector.reduce_sum(place[:, :], totals[:, :, :], axis=X_AXIS))
            link(nc.vector.tensor_copy(place_i[:, :], place[:, :]))
            nc.vector.tensor_single_scalar(place_parts[0][:, :], place_i[:, :], 7, op=ALU.logical_shift_right)
            link(nc.vector.tensor_single_scalar(place_parts[1][:, :], place_i[:, :], P - 1, op=ALU.bitwise_and))
            nc.vector.tensor_copy(place_tile[:, :], place_parts[0][:, :])
            link(nc.vector.tensor_copy(place_row[:, :], place_parts[1][:, :]))
            dve.wait_ge(xn_stored, 16 * 2 * B)
            dve.wait_ge(tr_ready, C * 2 * B)
            nc.vector.tensor_tensor(hot_tile, place_tile[:, :].unsqueeze(2).to_broadcast([P, 2 * NT, SLOTS]),
                                    slot_no[:, :, 0].unsqueeze(1).to_broadcast([P, 2 * NT, SLOTS]),
                                    ALU.is_equal).then_inc(hot_tile_ready, 1)
            for i in range(4):
                n = slice(8 * i, 8 * (i + 1))
                nc.vector.tensor_tensor(in_row[:, n, :],
                                        place_row[:, n].unsqueeze(2).to_broadcast([P, 8, P]),
                                        row_no[:, :].unsqueeze(1).to_broadcast([P, 8, P]), ALU.is_equal).then_inc(in_row_ready, 1)

            def rope_sum(q):
                if 1 <= q <= NP:
                    n, rows_q = (q - 1) % 3, part_rows(q - 1)
                    dve.wait_ge(cos_done, q)
                    dve.wait_ge(sin_done, q)
                    nc.vector.tensor_tensor(rope_a[n][0:rows_q, :], rope_a[n][0:rows_q, :],
                                            rope_b[n][0:rows_q, :], ALU.add).then_inc(rope_done, 1)

            def rope_step(q):
                if 2 <= q <= NP + 1:
                    n, rows_q = (q - 2) % 3, part_rows(q - 2)
                    dve.wait_ge(hi_ready, q - 1)
                    dve.wait_ge(rope_done, q - 1)
                    if q >= 5:
                        dve.wait_ge(qk_stored[n], stored_before(q - 2))
                    nc.vector.tensor_tensor(rope_lo[n][0:rows_q, :], rope_a[n][0:rows_q, :],
                                            rope_hi[n][0:rows_q, :].bitcast(F32), ALU.subtract).then_inc(lo_ready, 1)
                if q < NP:
                    (k, m), n, rows_q = PARTS[q], q % 3, part_rows(q)
                    if k < BLOCKS - 1:
                        dve.wait_ge(pj_copied, 3 * k + m + 1)
                    else:
                        dve.wait_ge(pj_ready, 3 * k + m + 1)
                    if q >= 3:
                        dve.wait_ge(rope_done, q - 2)
                    nc.vector.stream_shuffle(rope_b[n][0:rows_q, :], projected(k, m)[0:rows_q, :],
                                             [d ^ 1 for d in range(32)]).then_inc(swapped, 1)
                    if vector_cos(q):
                        dve.wait_ge(hi_ready, q - 2)
                        dve.wait_ge(lo_ready, q - 2)
                        nc.vector.tensor_tensor(rope_a[n][0:rows_q, :], projected(k, m)[0:rows_q, :],
                                                cos_s[0:rows_q, k % 2 * HALF:(k % 2 + 1) * HALF], ALU.mult).then_inc(cos_done, 1)

            rope_step(0)
            link(nc.vector.tensor_tensor(slot_ge[:, :, :], ends[:, :].unsqueeze(1).to_broadcast([P, SLOTS, E]),
                                         slot_no[:, :, :], ALU.is_le))
            link(nc.vector.reduce_sum(slot_e[:, :], slot_ge[:, :, :], axis=X_AXIS))
            nc.vector.tensor_scalar(slot_ei[:, :], slot_e[:, :], float(E - 1), None, ALU.min).then_inc(experts_known, 1)
            dve.wait_ge(inverse_ready, 1)
            link(nc.vector.tensor_copy(token_part[:, :], inverse_ps[:, 0:SLOTS]))
            nc.vector.tensor_tensor(token_of[:, :], inverse_ps[:, SLOTS:], token_part[:, :], ALU.add).then_inc(tokens_ready, 1)
            dve.wait_ge(gate_exp, 1)
            link(nc.vector.tensor_scalar(gate_t[:, 2, :], gate_t[:, 1, :], 1.0, None, ALU.add))
            link(nc.vector.reciprocal(gate[:, 0, :], gate_t[:, 2, :]))
            nc.vector.tensor_tensor(gate[:, 1, :], gate_t[:, 1, :], gate[:, 0, :], ALU.mult).then_inc(gates_ready, 1)
            for q in range(1, AHEAD):
                rope_sum(q)
                rope_step(q)

            def unit_max(h, a, n):
                i = a + (a >= TURN)
                dve.wait_ge(mx_scored, n + i + 1)
                nc.vector.reduce_max(mx[h][:, a // 2, a % 2:a % 2 + 1], mx_ps[i % 3], axis=X_AXIS).then_inc(mx_taken, 1)

            def join_maxima(h, uses):
                dve.wait_ge(mx_taken, uses)
                nc.vector.tensor_reduce(neg_mx[:, :], mx[h][:, :, :], X_AXIS, ALU.max, negate=True).then_inc(neg_mx_ready, 1)

            def split_maxima(v, h, n, i, sent):
                dve.wait_ge(mx_scored, n + i + 1)
                if sent is not None:
                    dve.wait_ge(qb_loaded[h], sent)
                turned = mx_ps[TURN % 3][0:R * QT, 0:P]
                nc.vector.tensor_copy(m_hi[h][:, :], turned).then_inc(m_hi_ready, 1)
                dve.wait_ge(m_hi_ready, v + 1)
                nc.vector.tensor_tensor(m_lo[h][:, :], turned, m_hi[h][:, :].bitcast(F32), ALU.subtract).then_inc(mx_taken, 1)

            def first_max(n):
                v, a = n // NA, n % NA
                if v:
                    if a == TURN:
                        split_maxima(0, 0, uses_before(1), TURN, None)
                    unit_max(1, a, uses_before(1))
                else:
                    dve.wait_ge(mx_scored, a + 1)
                    nc.vector.reduce_max(mx[0][:, a // 2, a % 2:a % 2 + 1], mx_ps[(a + (a >= TURN)) % 3],
                                         axis=X_AXIS).then_inc(mx_taken, 1)
                if a == NA - 1:
                    join_maxima(v, uses_before(1 + v))

            def expert(t, i):
                dve.wait_ge(silu_ready, t + 1)
                nc.vector.tensor_scalar(act_g[i], act_g[i], CLAMP, -CLAMP, ALU.min, ALU.max).then_inc(clip_done, 1)
                dve.wait_ge(clip_done, t + 1)
                nc.vector.tensor_tensor(act_h[i], gu_ps[i][:, F:2 * F], act_g[i], ALU.mult).then_inc(act_ready, 1)

            def take_y(t, q, i, stores, y=None):
                dve.wait_ge(y_ready, t + 1)
                if stores is not None:
                    dve.wait_ge(y_stored[q], stores)
                nc.vector.tensor_copy(y_s[q], y_ps[i] if y is None else y).then_inc(y_copied, 1)

            for t in range(NP):
                expert(t, t % 2)
                if t >= 2:
                    take_y(t - 2, (t - 2) % 4, t % 2, 16 * ((t - 2) // 4) if t >= 6 else None)
                rope_sum(t + AHEAD)
                rope_step(t + AHEAD)
            with dve.Fori(NP // 4, (SLOTS - SHARED) // 4) as j:
                for i in range(4):
                    expert(4 * j + i, i % 2)
                    take_y(4 * j + i - 2, (i + 2) % 4, i % 2, 16 * (j - 1 if i < 2 else j))
            for t in range(SLOTS - SHARED, SLOTS):
                todo = shared_with(t)
                for n in todo[0:2]:
                    first_max(n)
                expert(t, t % 2)
                for n in todo[2:3]:
                    first_max(n)
                take_y(t - 2, (t - 2) % 4, t % 2, 16 * ((t - 2) // 4))
                for n in todo[3:]:
                    first_max(n)
            for t in range(SLOTS - 2, SLOTS):
                take_y(t, t % 4, t % 2, 16 * (t // 4), last_y_ps if t == SLOTS - 1 else None)

            def turn_output(u, first=False):
                dve.wait_ge(products_done, KT * (u + 1))
                if not first:
                    dve.wait_ge(divided, u)
                nc.vector.transpose(o_q, o_ps).then_inc(o_free, 1)

            def invert_sums(u):
                dve.wait_ge(o_free, u + 2)
                nc.vector.reciprocal(rden[:, :], o_q.rearrange("p (n d) -> p n d", d=32)[:, :, HD]).then_inc(rden_ready, 1)

            def turn_back(g, h):
                dve.wait_ge(divided, 2 * g + h + 1)
                dve.wait_ge(o_t_free, g + h)
                nc.vector.transpose(o_t[h], o_n[h]).then_inc(attn_ready, 1)

            def group(g, p, first=False):
                for h in range(2):
                    u = 2 * g + h
                    n = uses_before(u + 2)
                    for a in range(NA):
                        if a == 1 and not (first and h == 0):
                            join_maxima(1 - h, n)
                        if a == 2 and not (first and h == 0):
                            invert_sums(u - 1)
                        if a == TURN:
                            split_maxima(u + 1, 1 - h, n, TURN, None if first and h == 0 else 64 * (g + h))
                        if a == NA - 8 and p == h and not (first and h == 0):
                            turn_back(g - 1 + h, 1 - h)
                        unit_max(h, a, n)
                    turn_output(u, first and h == 0)

            group(0, 0, first=True)
            group(1, 1)
            with dve.Fori(1, G // 2 - 1) as j:
                for p in range(2):
                    group(2 * j + p, p)
            group(G - 2, 0)
            u = 2 * G - 2
            join_maxima(1, uses_before(u + 2))
            invert_sums(u - 1)
            split_maxima(u + 1, 1, uses_before(u + 2), 0, 64 * (G - 1))

            def finish(n):
                for t in out_tiles(n):
                    dve.wait_ge(wo_ready, t + 1)
                    if t >= 4:
                        dve.wait_ge(stored[t % 4], 16 * (t // 4))
                    nc.vector.tensor_tensor(fin[t % 4], wo_ps[t % 3][:, 0:D], xs[:, t, :], ALU.add).then_inc(fin_ready, 1)

            dve.wait_ge(mix, 4 * NT)
            finish(0)
            turn_output(u)
            invert_sums(u)
            dve.wait_ge(divided, u + 1)
            nc.vector.transpose(attn_t[:, KC - 1, (B - 1) * S:(B - 1) * S + HALF], o_n[0]).then_inc(attn_ready, 1)
            finish(1)
            turn_output(u + 1)
            invert_sums(u + 1)
            dve.wait_ge(rden_ready, u + 2)
            nc.vector.tensor_tensor(side(o_n[1], 1), side(o_q, 0),
                                    rden[:, :].unsqueeze(2).to_broadcast([P, HALF // 32, HD]), ALU.mult).then_inc(divided, 1)
            dve.wait_ge(divided, u + 2)
            nc.vector.transpose(attn_t[:, KC - 1, (B - 1) * S + HALF:B * S], o_n[1]).then_inc(attn_ready, 1)
            finish(2)

        @block.tensor
        def _(pe):
            mm = nc.tensor.matmul
            pe.wait_ge(pool_made, 5)

            def columns(k):
                pe.wait_ge(xn_ready, 2 * (k + 1))
                for c in range(C):
                    if k:
                        pe.wait_ge(xn_t_ready, C * (k - 1) + c + 1)
                    for j in range(TB):
                        last = nc.tensor.transpose(tr_ps[c][:, j * P:(j + 1) * P],
                                                   xn[:, k * TB + j, c * P:(c + 1) * P], ident[:, :])
                    last.then_inc(tr_ready, 1)

            columns(0)
            pe.wait_ge(small_loaded, 16 * 6)
            for k in range(2 * B):
                if k < 2 * B - 1:
                    columns(k + 1)
                pe.wait_ge(xn_t_ready, C * (k + 1))
                for j in range(TB):
                    for c in range(C):
                        last = mm(vr_ps[k][:, j * NV:(j + 1) * NV], xn_t[k][:, c, j * P:(j + 1) * P], wvr[:, c, :],
                                  start=(c == 0), stop=(c == C - 1))
                last.then_inc(vr_ready, 1)

            def queries_keys(k, parts=(0, 1, 2)):
                for m in parts:
                    rows_m = (P, P, KV * HD)[m]
                    if k >= 2:
                        pe.wait_ge(pj_copied, 3 * (k - 2) + m + 1)
                    for c in range(C):
                        last = mm(pj_ps[k][m][0:rows_m, :], wqk[:, c, m * P:m * P + rows_m], xn_t[k][:, c, :],
                                  start=(c == 0), stop=(c == C - 1))
                    last.then_inc(pj_ready, 1)

            pe.wait_ge(vr_taken, 4 * B)
            queries_keys(0)
            pe.wait_ge(choices_ready, 1)
            hot = onehot[:, :, :, :].rearrange("p k t e -> p (k t e)")
            mm(rank_ps, earlier[:, :], hot, start=True, stop=True)
            mm(total_ps, ones[:, :], hot, start=True, stop=True).then_inc(counts_ready, 1)
            for k in range(1, 2 * B - 1):
                queries_keys(k)
            queries_keys(2 * B - 1, [0])
            pe.wait_ge(in_tile_ready, 2)
            for n in range(2 * NT):
                if n % 8 == 0:
                    pe.wait_ge(in_row_ready, n // 8 + 1)
                last = mm(inverse_ps, in_row[:, n, :], in_tile[:, n, :, :].rearrange("p s w -> p (s w)"),
                          start=(n == 0), stop=(n == 2 * NT - 1))
            last.then_inc(inverse_ready, 1)
            queries_keys(2 * B - 1, [1, 2])

            def score_max(h, p, a, i, taken):
                r, qt, kh = a // (2 * QT), a // 2 % QT, a % 2
                if taken is not None:
                    pe.wait_ge(mx_taken, taken)
                mm(mx_ps[i % 3], qa[h][:, r, qt * P:(qt + 1) * P], ka[p][:, kh * HALF:(kh + 1) * HALF],
                   start=True, stop=True).then_inc(mx_scored, 1)

            def turn_maxima(v, taken):
                pe.wait_ge(neg_mx_ready, v + 1)
                pe.wait_ge(mx_taken, taken)
                nc.tensor.transpose(mx_ps[TURN % 3][0:R * QT, 0:P], neg_mx[:, :], ident[:, :]).then_inc(mx_scored, 1)

            def first_max(n):
                v, a = n // NA, n % NA
                i = a + (a >= TURN)
                if a == 0:
                    pe.wait_ge(qa_loaded[v], 32)
                if v:
                    if a == TURN:
                        turn_maxima(0, uses_before(1) + TURN - 2)
                    score_max(1, 0, a, i, uses_before(1) + i - 2)
                else:
                    score_max(0, 0, a, i, a - 1 if a >= 2 else None)

            expert_reg = [pe.alloc_register(f"expert{i}") for i in range(4)]

            def load_expert(t, i):
                pe.reg_load(expert_reg[i], slot_ei[0:1, bass.ds(t, 1)])

            def expert_of(i):
                return pe.snap(expert_reg[i], min_val=0, max_val=E - 1)

            def to_columns(t, i):
                for c in range(C):
                    last = nc.tensor.transpose(xt_ps[i % 2][:, c * P:(c + 1) * P], rows[i][:, c * P:(c + 1) * P], ident[:, :])
                last.then_inc(xt_ready, 1)

            def gate_up(t, i, between):
                e = expert_of(i)
                pe.wait_ge(rows_t_ready, t + 1)
                for c in range(C):
                    if c:
                        for x in between:
                            first_max(x)
                    last = mm(gu_ps[i % 2][:, :], rows_t[i % 2][:, c, :], wgu[:, e, c, :], start=(c == 0), stop=(c == C - 1))
                last.then_inc(gu_ready, 1)

            def act_columns(t, i, reused=True):
                pe.wait_ge(act_ready, t + 1)
                if reused:
                    pe.wait_ge(act_t_ready, t)
                for c in range(C):
                    last = nc.tensor.transpose(ht_ps[i % 2][:, c * P:(c + 1) * P], act_h[i % 2][:, c * P:(c + 1) * P], ident[:, :])
                last.then_inc(ht_ready, 1)

            def down(t, i, reused, y=None):
                e = expert_of(i)
                if reused:
                    pe.wait_ge(y_copied, t)
                pe.wait_ge(act_t_ready, t + 1)
                for c in range(C):
                    last = mm(y_ps[i % 2] if y is None else y, act_t[i % 2][:, c, :], wdn[:, e, c, :], start=(c == 0), stop=(c == C - 1))
                last.then_inc(y_ready, 1)

            def expert(t, i, loads, first=False, last=False, beside=()):
                def products(n):
                    for x in n:
                        first_max(x)

                gate_up(t, i, beside[0:1])
                products(beside[1:2])
                if not last:
                    load_expert(t + 1, (i + 1) % 4)
                if not first:
                    act_columns(t - 1, i - 1, not isinstance(t, int) or t >= 2)
                if not last:
                    pe.wait_ge(rows_loaded[(i + 1) % 4], loads)
                    to_columns(t + 1, (i + 1) % 4)
                products(beside[2:3])
                if not isinstance(t, int) or t >= 2:
                    down(t - 2, (i - 2) % 4, not isinstance(t, int) or t >= 3)
                products(beside[3:])

            pe.wait_ge(experts_known, 1)
            load_expert(0, 0)
            pe.wait_ge(experts_loaded, 16 * 3 * C * E)
            pe.wait_ge(rows_loaded[0], 16)
            to_columns(0, 0)
            for t in range(NP):
                expert(t, t % 4, 16 * ((t + 1) // 4 + 1), first=t == 0)
            with pe.Fori(NP // 4, (SLOTS - SHARED) // 4) as j:
                for i in range(4):
                    expert(4 * j + i, i, 16 * (j + 1 + (i + 1) // 4))
            pe.wait_ge(stacks_padded, 10)
            pe.wait_ge(ka_loaded[0], 16)
            for t in range(SLOTS - SHARED, SLOTS):
                expert(t, t % 4, 16 * ((t + 1) // 4 + 1), last=t == SLOTS - 1, beside=shared_with(t))
            act_columns(SLOTS - 1, (SLOTS - 1) % 4)
            down(SLOTS - 2, (SLOTS - 2) % 4, True)
            down(SLOTS - 1, (SLOTS - 1) % 4, False, last_y_ps)

            def scores(h, p, kt, s, j):
                if s is not None:
                    pe.wait_ge(exp_done, 2 * (s - 1) + j + 1)
                for r in (2 * j, 2 * j + 1):
                    last = mm(st_ps[j][:, (r - 2 * j) * HALF:(r - 2 * j + 1) * HALF],
                              kb[p][:, kt * P:(kt + 1) * P], qb[h][:, r, :], start=True, stop=True)
                last.then_inc(st_ready, 1)

            def values(p, kt, s, u):
                pe.wait_ge(exp_done, 2 * (s + 1))
                if kt == 0:
                    pe.wait_ge(o_free, u + 1)
                for r in range(R):
                    last = mm(o_ps[32 * r:32 * (r + 1), :], v_st[p][:, kt, :], probs[kt % 2][:, r, :],
                              start=(kt == 0), stop=(kt == KT - 1))
                last.then_inc(products_done, 1)

            pe.wait_ge(kb_loaded[0], 16)
            pe.wait_ge(qb_loaded[0], 64)
            scores(0, 0, 0, None, 0)
            pe.wait_ge(y_copied, SLOTS)
            scores(0, 0, 0, None, 1)

            def project_tile(t, chunks):
                for c in chunks:
                    if c == 0:
                        if t >= 3:
                            pe.wait_ge(fin_ready, t - 2)
                        if t == 0:
                            pe.wait_ge(wo_loaded, 16 * 2 * R)
                            pe.wait_ge(o_t_free, 2 + 2 * (G - 2) // 2)
                            pe.wait_ge(mx_taken, uses_before(2 * G) + 1)
                    if c == KC - 1 and t == KT:
                        pe.wait_ge(attn_ready, G - 1)
                    if c == KC - 1 and t == KT + QT:
                        pe.wait_ge(attn_ready, G)
                    last = mm(wo_ps[t % 3][:, 0:D], attn_t[:, c, t * P:(t + 1) * P], wo_s[:, c, :],
                              start=(c == 0), stop=(c == KC - 1))
                if chunks[-1] == KC - 1:
                    last.then_inc(wo_ready, 1)

            def project(n, kt):
                jobs = [(t, c) for t in out_tiles(n) for c in range(KC)]
                for t, c in jobs[len(jobs) * kt // KT:len(jobs) * (kt + 1) // KT]:
                    project_tile(t, [c])

            def group(g, p, last):
                for h in range(2):
                    u = 2 * g + h
                    n = uses_before(u + 2)

                    def maximum(a):
                        if not last:
                            if a == TURN:
                                turn_maxima(u + 1, n + TURN - 2)
                            i = a + (a >= TURN)
                            score_max(h, 1 - p, a, i, n + i - 2)

                    for kt in range(KT):
                        s = KT * u + kt
                        if not last and kt == 0:
                            pe.wait_ge(qa_loaded[h], 32 * (g + 2))
                            if h == 0:
                                pe.wait_ge(ka_loaded[1 - p], 16 * ((g - p) // 2 + p) + 16)
                        if last and h == 0 and kt == 0:
                            turn_maxima(u + 1, n)
                        if kt == KT - 1 and h == 0:
                            pe.wait_ge(qb_loaded[1], 64 * (g + 1))
                        if kt == KT - 1 and h == 1 and not last:
                            pe.wait_ge(kb_loaded[1 - p], 16 * ((g - p) // 2 + p) + 16)
                            pe.wait_ge(qb_loaded[0], 64 * (g + 2))
                        for j in range(2):
                            maximum(4 * kt + j)
                            if kt < KT - 1:
                                scores(h, p, kt + 1, s + 1, j)
                            elif h == 0:
                                scores(1, p, 0, s + 1, j)
                            elif not last:
                                scores(0, 1 - p, 0, s + 1, j)
                        maximum(4 * kt + 2)
                        maximum(4 * kt + 3)
                        if last:
                            project(h, kt)
                        if h == 0 and kt == 0:
                            pe.wait_ge(v_staged, g + 1)
                        values(p, kt, s, u)

            with pe.Fori(0, G // 2 - 1) as j:
                for p in range(2):
                    group(2 * j + p, p, False)
            group(G - 2, 0, False)
            group(G - 1, 1, True)

            early = out_tiles(2)[0:3]
            for t in early:
                project_tile(t, [0])
            for t in out_tiles(2):
                project_tile(t, [1] if t in early else [0, 1])


def rope_tables(seq):
    half = HD // 2
    freqs = (np.float32(1.0) / np.power(np.float32(10000.0), np.arange(half, dtype=np.float32) / np.float32(half))).astype(np.float32)
    angles = np.arange(seq, dtype=np.float32)[:, None] * freqs[None, :]
    dims = np.arange(P) % HD
    sign = np.where(dims % 2 == 0, -1.0, 1.0).astype(np.float32)
    cos_t = np.cos(angles)[:, dims // 2].T
    sin_t = np.sin(angles)[:, dims // 2].T * sign[:, None]
    return np.ascontiguousarray(cos_t, np.float32), np.ascontiguousarray(sin_t, np.float32)


NAMES = ["L0_attn_x", "L0_attn_W_q", "L0_attn_W_k", "L0_attn_W_v", "L0_attn_W_o",
         "L0_ffn_Wr", "L0_ffn_Wg", "L0_ffn_Wu", "L0_ffn_Wd"]


def kernel(**inputs):
    import concourse.bacc as bacc
    from concourse.bass_utils import run_bass_kernel_spmd

    nc = bacc.Bacc("TRN2", target_bir_lowering=False, num_devices=1)
    arrays = {f"in_{n}": np.ascontiguousarray(inputs[n]) for n in NAMES}
    seq = arrays["in_L0_attn_x"].shape[1]
    arrays["rope_cos"], arrays["rope_sin"] = rope_tables(seq)
    args = [nc.dram_tensor(n, a.shape, F32, kind="ExternalInput").ap() for n, a in arrays.items()]
    out = nc.dram_tensor("out", arrays["in_L0_attn_x"].shape, F32, kind="ExternalOutput").ap()
    build(nc, *args, out)
    r = run_bass_kernel_spmd(nc, [arrays], core_ids=[0])
    return r.results[0]["out"]
```
